# Optimizing a Trainium2 kernel written in Bass

```python
import numpy as np
import jax
import jax.numpy as jnp

def _softmax(x, axis=-1):
    return jax.nn.softmax(x, axis=axis)
def _gelu(x):
    return jax.nn.gelu(x, approximate=True)
def _silu(x):
    return jax.nn.silu(x)
def _sigmoid(x):
    return jax.nn.sigmoid(x)
def _layernorm(x, axis=-1, eps=1e-5):
    m = jnp.mean(x, axis=axis, keepdims=True)
    v = jnp.var(x, axis=axis, keepdims=True)
    return (x - m) / jnp.sqrt(v + eps)
def _scatter_add(tgt, idx, src, axis=0):
    return tgt.at[idx].add(src)
def _segment_sum(src, seg, n):
    return jax.ops.segment_sum(src, seg, n)

kernel_name = 'mk_conv_seq_d1_conv_nhwc512_a6ee92'

def setup_inputs(seed: int = 0):
    np.random.seed(seed)
    _w = jnp.asarray
    def _rec_inputs():
        import jax
        import jax.numpy as jnp
        _gk = jax.random.key(seed)
        x = 7.22e-05 + 1 * jax.random.normal(jax.random.fold_in(_gk, 1), (16, 32, 32, 512), jnp.float32)
        return x
    x = _rec_inputs()
    def _L0_conv_setup():
        import jax, jax.numpy as jnp
        import numpy as np
        N_HEADS = 8
        D_HEAD = 64
        SCALE = D_HEAD ** (-0.5)
        key = jax.random.key(seed)
        k1, k2, k3 = jax.random.split(key, 3)
        B, H, W, C = (16, 32, 32, 512)
        ft = jax.random.normal(k1, (B, H, W, C), dtype=jnp.float32)
        w_qkv = jax.random.normal(k2, (C, N_HEADS * D_HEAD * 3), dtype=jnp.float32) * C ** (-0.5)
        b_qkv = jnp.zeros((N_HEADS * D_HEAD * 3,), dtype=jnp.float32)
        w_out = jax.random.normal(k3, (N_HEADS * D_HEAD, C), dtype=jnp.float32) * (N_HEADS * D_HEAD) ** (-0.5)
        b_out = jnp.zeros((C,), dtype=jnp.float32)
        return {'ft': ft, 'w_qkv': w_qkv, 'b_qkv': b_qkv, 'w_out': w_out, 'b_out': b_out}
    _L0_conv_all = _L0_conv_setup()
    _L0_conv_in = {k: v for k, v in _L0_conv_all.items() if k in ('w_qkv', 'b_qkv', 'w_out', 'b_out', )}
    del _L0_conv_all

    return {
        "x": x,
        "L0_conv_w_qkv": _L0_conv_in["w_qkv"],
        "L0_conv_b_qkv": _L0_conv_in["b_qkv"],
        "L0_conv_w_out": _L0_conv_in["w_out"],
        "L0_conv_b_out": _L0_conv_in["b_out"],
    }

def reference(x, L0_conv_w_qkv, L0_conv_b_qkv, L0_conv_w_out, L0_conv_b_out):
    import jax
    import jax.numpy as jnp
    def _L0_conv_ref(ft, w_qkv, b_qkv, w_out, b_out):
        import jax, jax.numpy as jnp
        import numpy as np
        N_HEADS = 8
        D_HEAD = 64
        SCALE = D_HEAD ** (-0.5)
        B, H, W, C = ft.shape
        N = H * W
        x = ft.reshape(B, N, C)
        qkv = x @ w_qkv + b_qkv
        qkv = qkv.reshape(B, N, N_HEADS, 3 * D_HEAD)
        q, k, v = jnp.split(qkv, 3, axis=-1)
        attn = jnp.einsum('bxhd,byhd->bxyh', q, k) * SCALE
        attn = jax.nn.softmax(attn, axis=2)
        res = jnp.einsum('bxyh,byhd->bxhd', attn, v)
        res = res.reshape(B, N, N_HEADS * D_HEAD)
        res = res @ w_out + b_out
        res = res + x
        return res.reshape(B, H, W, C)

    def _gn(v, G=32, eps=1e-5):
        B_, H_, W_, C_ = v.shape
        g = v.reshape(B_, H_, W_, G, C_ // G)
        m = jnp.mean(g, axis=(1, 2, 4), keepdims=True)
        s = jnp.var(g, axis=(1, 2, 4), keepdims=True)
        return ((g - m) / jnp.sqrt(s + eps)).reshape(v.shape)

    def _ln_c(v, eps=1e-6):
        m = jnp.mean(v, axis=-1, keepdims=True)
        s = jnp.var(v, axis=-1, keepdims=True)
        return (v - m) / jnp.sqrt(s + eps)

    def _ln_t(v, eps=1e-5):
        m = jnp.mean(v, axis=-1, keepdims=True)
        s = jnp.var(v, axis=-1, keepdims=True)
        return (v - m) / jnp.sqrt(s + eps)

    def _to_tokens(v):
        B_, H_, W_, C_ = v.shape
        return v.reshape(B_, H_ * W_, C_)
    def _from_tokens(t, like):
        return t.reshape(like.shape)

    x = _L0_conv_ref(x, L0_conv_w_qkv, L0_conv_b_qkv, L0_conv_w_out, L0_conv_b_out)
    return x


_drawn_inputs = setup_inputs


def setup_inputs(seed=0):
    import zlib

    import numpy as np

    out = dict(_drawn_inputs(seed))
    spreads = {'L0_conv_b_qkv': (0.0, 0.1), 'L0_conv_b_out': (0.0, 0.1)}
    factors = {}
    for name, (base, spread) in spreads.items():
        noise = np.random.default_rng([zlib.crc32(name.encode()), seed]).standard_normal(out[name].shape)
        drawn = base * np.exp(spread * noise) if base else spread * noise
        out[name] = jnp.asarray(drawn.astype(out[name].dtype))
    for name, factor in factors.items():
        out[name] = (out[name] * factor).astype(out[name].dtype)
    return out
```

```python
from contextlib import ExitStack

import concourse.bass as bass
from concourse import mybir

P = 128
BATCH, HEIGHT, WIDTH, CH = 16, 32, 32, 512
TOKENS = HEIGHT * WIDTH
HEADS, DIM = 8, 64
SCALE = DIM ** -0.5
QKV = 3 * DIM
TOKEN_TILES = TOKENS // P
CH_TILES = CH // P
HALF = 512
HALVES = TOKENS // HALF
Q_TILES = HALF // P
UNITS = HEADS * HALVES
STEPS_PER_UNIT = 4
STEPS = UNITS * STEPS_PER_UNIT
KEYS_PER_STEP = TOKENS // STEPS_PER_UNIT // P
V_WIDTH = 2 * DIM + 2
X_SLOTS, Y_SLOTS, P_SLOTS = 4, 4, 3
FIRST_SLOT = -9
LAST_SLOT = STEPS + 1
W_CHUNKS = 3 * HEADS * DIM // HALF


def works_before_attention():
    order = [("x_transpose", 0)]
    for t in range(TOKEN_TILES):
        if t + 1 < TOKEN_TILES:
            order.append(("x_transpose", t + 1))
        order.append(("v", t))
    return order


def works_of_slot(s):
    works = []
    if 0 <= (s + 6) // 4 < UNITS:
        unit, q_tile = divmod(s + 6, 4)
        works += [("row_max", unit, q_tile, k_half) for k_half in range(2)]
    if (s + 2) % 4 == 0 and 0 <= (s + 2) // 4 < UNITS:
        works.append(("shift", (s + 2) // 4))
    if (s + 1) % 8 == 0 and (s + 1) // 8 + 1 < HEADS:
        works.append(("qk", (s + 1) // 8 + 1, 0))
    if s % 8 == 0 and s // 8 + 1 < HEADS:
        works.append(("qk", s // 8 + 1, 1))
    return works


def works_after_attention():
    order = [("o_transpose", 0)]
    for t in range(TOKEN_TILES):
        if t + 1 < TOKEN_TILES:
            order.append(("o_transpose", t + 1))
        order.append(("project", t))
    return order


WORK_ORDER = (works_before_attention()
              + [w for s in range(FIRST_SLOT, LAST_SLOT + 1) for w in works_of_slot(s)]
              + works_after_attention())
WORKS = len(WORK_ORDER)
WORK_AT = {w: n for n, w in enumerate(WORK_ORDER)}
HI_ORDER = [w for w in WORK_ORDER if w[0] in ("x_transpose", "qk", "o_transpose")]
HIS = len(HI_ORDER)
HI_AT = {w: n for n, w in enumerate(HI_ORDER)}


def attention_block(nc: bass.Bass, x, w_qkv, b_qkv, w_out, b_out, out):
    f32, f32r, f16 = mybir.dt.float32, mybir.dt.float32r, mybir.dt.float16
    ALU, ACT, AX = mybir.AluOpType, mybir.ActivationFunctionType, mybir.AxisListType
    assert WORKS % 2 == 0

    x_tok = x.rearrange("b h w c -> b (h w) c")
    out_tok = out.rearrange("b h w c -> b (h w) c")

    with ExitStack() as ctx:
        def sb(name, shape, dt):
            return ctx.enter_context(nc.sbuf_tensor(name, shape, dt))

        def sem(name):
            return ctx.enter_context(nc.semaphore(name))

        wqkv_hi = sb("wqkv_hi", [P, CH_TILES, HEADS * QKV], f32r)
        wqkv_lo = sb("wqkv_lo", [P, CH_TILES, HEADS * QKV], f32r)
        wout_hi = sb("wout_hi", [P, CH_TILES, CH], f32r)
        wout_lo = sb("wout_lo", [P, CH_TILES, CH], f32r)
        xT_hi = sb("xT_hi", [P, CH_TILES, TOKENS], f32r)
        xT_lo = sb("xT_lo", [P, CH_TILES, TOKENS], f32r)
        x_in = sb("x_in", [P, X_SLOTS, CH], f32)
        o_heads = sb("o_heads", [P, TOKEN_TILES, CH], f32)
        v_parts = sb("v_parts", [P, TOKEN_TILES, HEADS, V_WIDTH], f16)
        v_full = sb("v_full", [P, CH], f32)
        k_lo_hi = sb("k_lo_hi", [P, 2, TOKENS], f32r)
        k_shift = sb("k_shift", [P, 2, TOKENS], f32r)
        q_hi_hi = sb("q_hi_hi", [P, 2, TOKENS], f32r)
        q_shift = sb("q_shift", [P, 2, TOKENS], f32r)
        p_full = sb("p_full", [P, 2, KEYS_PER_STEP, HALF], f32)
        p_hi = sb("p_hi", [P, P_SLOTS, KEYS_PER_STEP, HALF], f16)
        p_lo = sb("p_lo", [P, P_SLOTS, KEYS_PER_STEP, HALF], f16)
        y_tile = sb("y_tile", [P, Y_SLOTS, CH], f32)
        identity = sb("identity", [P, P], f32)
        qk_bias = sb("qk_bias", [P, HEADS], f32)
        v_bias = sb("v_bias", [P, HEADS, DIM], f32)
        out_bias = sb("out_bias", [P, CH], f32)
        minus_block = sb("minus_block", [Q_TILES, Q_TILES, P], f32)
        max_parts = sb("max_parts", [P, 2, Q_TILES, 2], f32)
        row_max = sb("row_max", [P, 2, Q_TILES], f32)
        o_lo = sb("o_lo", [P, Q_TILES, DIM], f32)
        o_sum = sb("o_sum", [P, Q_TILES, DIM], f32)
        inv_sum = sb("inv_sum", [P, Q_TILES], f32)
        stage = o_heads

        scores = ctx.enter_context(nc.psum_tensor("scores", [P, 2, KEYS_PER_STEP, HALF], f32))
        work = ctx.enter_context(nc.psum_tensor("work", [P, 2, HALF], f32))
        pv = ctx.enter_context(nc.psum_tensor("pv", [P, 2, HALF], f32))
        PV_W = 2 * DIM + 1

        weights_in = sem("weights_in")
        consts_in = sem("consts_in")
        w_hi_done = sem("w_hi_done")
        w_lo_done = sem("w_lo_done")
        consts_ready = sem("consts_ready")
        fills = sem("fills")
        x_loaded = [sem(f"x_loaded{k}") for k in range(X_SLOTS)]
        y_loaded = [sem(f"y_loaded{k}") for k in range(Y_SLOTS)]
        y_stored = [sem(f"y_stored{k}") for k in range(Y_SLOTS)]
        y_biased = sem("y_biased")
        work_ready = sem("work_ready")
        work_done = sem("work_done")
        hi_done = sem("hi_done")
        k_shift_ready = [sem(f"k_shift_ready{k}") for k in range(HALVES)]
        scores_ready = sem("scores_ready")
        p_full_ready = sem("p_full_ready")
        p_hi_ready = sem("p_hi_ready")
        p_lo_ready = sem("p_lo_ready")
        pv_done = sem("pv_done")
        max_ready = sem("max_ready")
        o_lo_ready = sem("o_lo_ready")
        o_free = sem("o_free")
        o_ready = sem("o_ready")
        dve_chain = sem("dve_chain")

        block = ctx.enter_context(nc.Block())

        def key_tile(step, n):
            return KEYS_PER_STEP * (step % STEPS_PER_UNIT) + n

        @block.sync
        def _(sp):
            w_view = w_qkv.rearrange("(c p) n -> p c n", p=P)
            wo_view = w_out.rearrange("(c p) n -> p c n", p=P)
            for c in range(CH_TILES):
                for n in range(2):
                    sp.dma_start(stage[:, 2 * c + n, :], w_view[:, c, n * HALF:(n + 1) * HALF]).then_inc(weights_in, 16)
            with nc.allow_non_contiguous_dma(reason="biases, once"):
                sp.dma_start(qk_bias[:, :], b_qkv.rearrange("(h e) -> e h", e=QKV)[0:P, :]).then_inc(consts_in, 16)
            sp.dma_start(v_bias[:, :, :],
                         b_qkv.rearrange("(o h e) -> o h e", o=1, e=QKV)[:, :, 2 * DIM:QKV].broadcast_to([P, HEADS, DIM])).then_inc(consts_in, 16)
            sp.dma_start(out_bias[:, :], b_out.rearrange("(o n) -> o n", o=1).broadcast_to([P, CH])).then_inc(consts_in, 16)
            for t in range(X_SLOTS):
                sp.dma_start(x_in[:, t, :], x_tok[0, t * P:(t + 1) * P, :]).then_inc(x_loaded[t], 16)
            sp.wait_ge(w_lo_done, 8)
            for c in range(CH_TILES):
                sp.dma_start(stage[:, c, :], w_view[:, c, 2 * HALF:3 * HALF]).then_inc(weights_in, 16)
                sp.dma_start(stage[:, 4 + c, :], wo_view[:, c, :]).then_inc(weights_in, 16)

            def batch(i, last):
                for k in range(Y_SLOTS):
                    sp.wait_ge(y_stored[k], i * 32)
                for t in range(X_SLOTS, TOKEN_TILES):
                    sp.wait_ge(work_ready, i * WORKS + WORK_AT["x_transpose", t - X_SLOTS] + 1)
                    sp.dma_start(x_in[:, t % X_SLOTS, :], x_tok[i, t * P:(t + 1) * P, :]).then_inc(x_loaded[t % X_SLOTS], 16)
                for h in range(HEADS):
                    for half in range(HALVES):
                        cols = slice(half * HALF, (half + 1) * HALF)
                        sp.wait_ge(hi_done, i * HIS + HI_AT["qk", h, half] + 1)
                        sp.dma_start(k_shift[DIM:P, h % 2, cols].bitcast(f32),
                                     k_lo_hi[DIM:P, h % 2, cols].bitcast(f32)).then_inc(k_shift_ready[half], 16)
                if not last:
                    for t in range(X_SLOTS):
                        sp.wait_ge(work_ready, i * WORKS + WORK_AT["x_transpose", t + X_SLOTS] + 1)
                        sp.dma_start(x_in[:, t, :], x_tok[i + 1, t * P:(t + 1) * P, :]).then_inc(x_loaded[t], 16)
                for t in range(TOKEN_TILES + Y_SLOTS):
                    if t >= Y_SLOTS:
                        done = t - Y_SLOTS
                        sp.wait_ge(work_done, i * WORKS + WORK_AT["project", done] + 1)
                        sp.dma_start(out_tok[i, done * P:(done + 1) * P, :], y_tile[:, done % Y_SLOTS, :]).then_inc(y_stored[done % Y_SLOTS], 16)
                    if t < TOKEN_TILES:
                        if t >= Y_SLOTS:
                            sp.wait_ge(y_stored[t % Y_SLOTS], i * 32 + 16)
                        sp.dma_start(y_tile[:, t % Y_SLOTS, :], x_tok[i, t * P:(t + 1) * P, :]).then_inc(y_loaded[t % Y_SLOTS], 16)

            with sp.Fori(0, BATCH - 1) as i:
                batch(i, False)
            batch(BATCH - 1, True)
            for k in range(Y_SLOTS):
                sp.wait_ge(y_stored[k], BATCH * 32)

        @block.gpsimd
        def _(pool):
            nc.gpsimd.memset(identity[:, :], 0.0).then_inc(consts_ready, 1)
            nc.gpsimd.memset(minus_block[:, :, :], 0.0).then_inc(consts_ready, 1)
            pool.wait_ge(consts_ready, 2)
            nc.gpsimd.affine_select(out=identity[:, :], in_=identity[:, :], compare_op=ALU.not_equal, fill=1.0,
                                    base=0, pattern=[[-1, P]], channel_multiplier=1).then_inc(consts_ready, 1)
            nc.gpsimd.affine_select(out=minus_block[:, :, :], in_=minus_block[:, :, :], compare_op=ALU.not_equal,
                                    fill=-1.0, base=0, pattern=[[-1, Q_TILES], [0, P]],
                                    channel_multiplier=1).then_inc(consts_ready, 1)
            pool.wait_ge(consts_in, 48)
            with pool.Fori(0, BATCH) as i:
                for t in range(TOKEN_TILES):
                    pool.wait_ge(y_loaded[t % Y_SLOTS], i * 32 + 16 * (t // Y_SLOTS + 1))
                    nc.gpsimd.tensor_tensor(y_tile[:, t % Y_SLOTS, :], y_tile[:, t % Y_SLOTS, :], out_bias[:, :],
                                            ALU.add).then_inc(y_biased, 1)

        @block.tensor
        def _(pe):
            pe.wait_ge(consts_ready, 4)
            pe.wait_ge(w_lo_done, 16)
            pe.wait_ge(fills, 1)

            with pe.Fori(0, BATCH) as i:
                def claim(w):
                    n = WORK_AT[w]
                    pe.wait_ge(work_done, i * WORKS + max(n - 1, 0))
                    return work[:, n % 2, :]

                def split_product(dst, terms):
                    for n, (a, b) in enumerate(terms):
                        last = nc.tensor.matmul(dst, a, b, start=n == 0, stop=n == len(terms) - 1)
                    last.then_inc(work_ready, 1)

                def three_terms(a_hi, a_lo, b_hi, b_lo):
                    return [pair for c in range(CH_TILES) for pair in
                            ((a_hi(c), b_hi(c)), (a_hi(c), b_lo(c)), (a_lo(c), b_hi(c)))]

                def x_transpose(t):
                    dst = claim(("x_transpose", t))
                    pe.wait_ge(x_loaded[t % X_SLOTS], i * 32 + 16 * (t // X_SLOTS + 1))
                    for c in range(CH_TILES):
                        last = nc.tensor.transpose(dst[:, c * P:(c + 1) * P], x_in[:, t % X_SLOTS, c * P:(c + 1) * P],
                                                   identity[:, :])
                    last.then_inc(work_ready, 1)

                def v_tile(t):
                    dst = claim(("v", t))
                    pe.wait_ge(work_done, i * WORKS + WORK_AT["x_transpose", t] + 1)
                    toks = slice(t * P, (t + 1) * P)

                    def v_cols(w):
                        return lambda c: w[:, c, :].rearrange("p (h e) -> p h e", e=QKV)[:, :, 2 * DIM:QKV]
                    split_product(dst, three_terms(lambda c: xT_hi[:, c, toks], lambda c: xT_lo[:, c, toks],
                                                   v_cols(wqkv_hi), v_cols(wqkv_lo)))

                def qk_tile(h, half):
                    dst = claim(("qk", h, half))
                    toks = slice(half * HALF, (half + 1) * HALF)
                    cols = slice(h * QKV, h * QKV + 2 * DIM)
                    split_product(dst, three_terms(lambda c: wqkv_hi[:, c, cols], lambda c: wqkv_lo[:, c, cols],
                                                   lambda c: xT_hi[:, c, toks], lambda c: xT_lo[:, c, toks]))

                def row_max_tile(u, q_tile, k_half):
                    h, half = divmod(u, HALVES)
                    dst = claim(("row_max", u, q_tile, k_half))
                    pe.wait_ge(work_done, i * WORKS + WORK_AT["qk", h, 1] + 1)
                    q0 = half * HALF + q_tile * P
                    split_product(dst, [(q_hi_hi[:, h % 2, q0:q0 + P],
                                         k_lo_hi[:, h % 2, k_half * HALF:(k_half + 1) * HALF])])

                def shift_tile(u):
                    dst = claim(("shift", u))
                    pe.wait_ge(max_ready, i * UNITS + u + 1)
                    nc.tensor.transpose(dst[0:Q_TILES, 0:P], row_max[:, u % 2, :], identity[:, :]).then_inc(work_ready, 1)

                def o_transpose(t):
                    dst = claim(("o_transpose", t))
                    if t == 0:
                        pe.wait_ge(o_ready, i * UNITS + UNITS)
                    for c in range(CH_TILES):
                        last = nc.tensor.transpose(dst[:, c * P:(c + 1) * P], o_heads[:, t, c * P:(c + 1) * P],
                                                   identity[:, :])
                    last.then_inc(work_ready, 1)

                def project(t):
                    dst = claim(("project", t))
                    pe.wait_ge(work_done, i * WORKS + WORK_AT["o_transpose", t] + 1)
                    toks = slice(t * P, (t + 1) * P)
                    split_product(dst, three_terms(lambda c: xT_hi[:, c, toks], lambda c: xT_lo[:, c, toks],
                                                   lambda c: wout_hi[:, c, :], lambda c: wout_lo[:, c, :]))

                kinds = {"x_transpose": x_transpose, "v": v_tile, "qk": qk_tile, "row_max": row_max_tile,
                         "shift": shift_tile, "o_transpose": o_transpose, "project": project}

                def step_scores(s):
                    u = s // STEPS_PER_UNIT
                    h, half = divmod(u, HALVES)
                    if s % STEPS_PER_UNIT == 0:
                        pe.wait_ge(work_done, i * WORKS + WORK_AT["shift", u] + 1)
                        if half == 0:
                            for k in range(HALVES):
                                pe.wait_ge(k_shift_ready[k], (i * HEADS + h + 1) * 16)
                    pe.wait_ge(p_hi_ready, i * STEPS + max(s - 1, 0))
                    cols = slice(half * HALF, (half + 1) * HALF)
                    for n in range(KEYS_PER_STEP):
                        keys = slice(key_tile(s, n) * P, (key_tile(s, n) + 1) * P)
                        dst = scores[:, s % 2, n, :]
                        nc.tensor.matmul(dst, k_lo_hi[:, h % 2, keys], q_hi_hi[:, h % 2, cols], start=True, stop=False)
                        last = nc.tensor.matmul(dst, k_shift[:, h % 2, keys], q_shift[:, h % 2, cols],
                                                start=False, stop=True)
                    last.then_inc(scores_ready, 1)

                def step_pv(s):
                    u = s // STEPS_PER_UNIT
                    h = u // HALVES
                    if s % STEPS_PER_UNIT == 0:
                        pe.wait_ge(o_free, i * UNITS + u)
                    pe.wait_ge(p_hi_ready, i * STEPS + s + 1)
                    pe.wait_ge(p_lo_ready, i * STEPS + s + 1)
                    for n in range(KEYS_PER_STEP):
                        kt = key_tile(s, n)
                        for qt in range(Q_TILES):
                            bank, col = qt // 2, (qt % 2) * PV_W
                            qs = slice(qt * P, (qt + 1) * P)
                            nc.tensor.matmul(pv[:, bank, col:col + PV_W], p_hi[:, s % P_SLOTS, n, qs],
                                             v_parts[:, kt, h, 0:PV_W], start=kt == 0 and qt % 2 == 0,
                                             stop=False, skip_group_check=True)
                            last = nc.tensor.matmul(pv[:, bank, col + DIM:col + PV_W], p_lo[:, s % P_SLOTS, n, qs],
                                                    v_parts[:, kt, h, DIM:PV_W], start=False,
                                                    stop=kt == TOKEN_TILES - 1, skip_group_check=True)
                    last.then_inc(pv_done, 1)

                for w in works_before_attention():
                    kinds[w[0]](*w[1:])
                for s in range(FIRST_SLOT, STEPS + 1):
                    if 0 <= s + 1 < STEPS:
                        step_scores(s + 1)
                    for w in works_of_slot(s):
                        kinds[w[0]](*w[1:])
                    if s >= 1:
                        step_pv(s - 1)
                for w in works_after_attention():
                    kinds[w[0]](*w[1:])

        @block.scalar
        def _(act):
            for n in range(2 * TOKEN_TILES):
                rnd, slot = divmod(n, 8)
                if slot == 0:
                    act.wait_ge(weights_in, 128 * (rnd + 1))
                if rnd == 0:
                    c, part = divmod(slot, 2)
                    dst = wqkv_hi[:, c, part * HALF:(part + 1) * HALF]
                elif slot < CH_TILES:
                    dst = wqkv_hi[:, slot, 2 * HALF:3 * HALF]
                else:
                    dst = wout_hi[:, slot - CH_TILES, :]
                nc.scalar.copy(dst, stage[:, slot, :]).then_inc(w_hi_done, 1)
            act.wait_ge(consts_in, 48)

            with act.Fori(0, BATCH) as i:
                def transposed_hi(w):
                    t, n = w[1], WORK_AT[w]
                    act.wait_ge(work_ready, i * WORKS + n + 1)
                    nc.scalar.copy(xT_hi[:, :, t * P:(t + 1) * P],
                                   work[:, n % 2, :].rearrange("p (c k) -> p c k", c=CH_TILES)).then_inc(hi_done, 1)

                def qk_hi(h, half):
                    n = WORK_AT["qk", h, half]
                    cols = slice(half * HALF, (half + 1) * HALF)
                    act.wait_ge(work_ready, i * WORKS + n + 1)
                    q, k = work[0:DIM, n % 2, :], work[DIM:P, n % 2, :]
                    nc.scalar.activation(q_hi_hi[0:DIM, h % 2, cols], q, ACT.Identity, bias=qk_bias[0:DIM, h:h + 1])
                    nc.scalar.activation(q_hi_hi[DIM:P, h % 2, cols], q, ACT.Identity, bias=qk_bias[0:DIM, h:h + 1])
                    nc.scalar.activation(k_lo_hi[DIM:P, h % 2, cols], k, ACT.Identity,
                                         bias=qk_bias[DIM:P, h:h + 1]).then_inc(hi_done, 1)

                def step_exp(s):
                    act.wait_ge(scores_ready, i * STEPS + s + 1)
                    act.wait_ge(p_lo_ready, i * STEPS + max(s - 1, 0))
                    nc.scalar.activation(p_full[:, s % 2, :, :], scores[:, s % 2, :, :], ACT.Exp,
                                         scale=SCALE).then_inc(p_full_ready, 1)
                    act.wait_ge(pv_done, i * STEPS + max(s + 1 - P_SLOTS, 0))
                    nc.scalar.activation(p_hi[:, s % P_SLOTS, :, :], scores[:, s % 2, :, :], ACT.Exp,
                                         scale=SCALE).then_inc(p_hi_ready, 1)

                def unit_lo(u):
                    act.wait_ge(pv_done, i * STEPS + STEPS_PER_UNIT * (u + 1))
                    act.wait_ge(o_free, i * UNITS + u)
                    for bank in range(2):
                        last = nc.scalar.copy(o_lo[:, 2 * bank:2 * bank + 2, :],
                                              pv[:, bank, 0:2 * PV_W].rearrange("p (t e) -> p t e", e=PV_W)[:, :, 0:DIM])
                    last.then_inc(o_lo_ready, 1)

                for w in works_before_attention():
                    if w[0] == "x_transpose":
                        transposed_hi(w)
                for s in range(FIRST_SLOT, LAST_SLOT + 1):
                    if s >= 5 and s % STEPS_PER_UNIT == 1:
                        unit_lo((s - 5) // STEPS_PER_UNIT)
                    if 0 <= s < STEPS:
                        step_exp(s)
                    for w in works_of_slot(s):
                        if w[0] == "qk":
                            qk_hi(*w[1:])
                for w in works_after_attention():
                    if w[0] == "o_transpose":
                        transposed_hi(w)

        @block.vector
        def _(dve):
            nc.vector.memset(k_shift[0:DIM, :, :].bitcast(f32), 0.0).then_inc(dve_chain, 1)
            nc.vector.memset(q_shift[0:DIM, :, :].bitcast(f32), 0.0)
            nc.vector.memset(v_parts[:, :, :, 2 * DIM:V_WIDTH], 1.0)
            dve.wait_ge(dve_chain, 1)
            nc.vector.memset(k_shift[0:Q_TILES, :, :].bitcast(f32), 1.0).then_inc(fills, 1)
            for n in range(2 * TOKEN_TILES):
                rnd, slot = divmod(n, 8)
                dve.wait_ge(w_hi_done, n + 1)
                if rnd == 0:
                    c, part = divmod(slot, 2)
                    where = (slice(None), c, slice(part * HALF, (part + 1) * HALF))
                    hi, lo = wqkv_hi[where], wqkv_lo[where]
                elif slot < CH_TILES:
                    where = (slice(None), slot, slice(2 * HALF, 3 * HALF))
                    hi, lo = wqkv_hi[where], wqkv_lo[where]
                else:
                    hi, lo = wout_hi[:, slot - CH_TILES, :], wout_lo[:, slot - CH_TILES, :]
                nc.vector.tensor_tensor(lo, stage[:, slot, :], hi.bitcast(f32), ALU.subtract).then_inc(w_lo_done, 1)
            dve.wait_ge(consts_in, 48)
            dve.wait_ge(consts_ready, 4)
            V_LINKS = 2
            LINKS = V_LINKS * TOKEN_TILES

            with dve.Fori(0, BATCH) as i:
                linked = [0]

                def link(ins):
                    ins.then_inc(dve_chain, 1)
                    linked[0] += 1
                    dve.wait_ge(dve_chain, i * LINKS + 1 + linked[0])

                def ready(w):
                    n = WORK_AT[w]
                    dve.wait_ge(work_ready, i * WORKS + n + 1)
                    return work[:, n % 2, :]

                def transposed_lo(w):
                    t, src = w[1], ready(w)
                    dve.wait_ge(hi_done, i * HIS + HI_AT[w] + 1)
                    toks = slice(t * P, (t + 1) * P)
                    nc.vector.tensor_tensor(xT_lo[:, :, toks], src.rearrange("p (c k) -> p c k", c=CH_TILES),
                                            xT_hi[:, :, toks].bitcast(f32), ALU.subtract).then_inc(work_done, 1)

                def v_split(t):
                    src = ready(("v", t))
                    full = v_full[:, :].rearrange("p (h d) -> p h d", d=DIM)
                    dve.wait_ge(work_done, i * WORKS + (WORK_AT["v", t - 1] + 1 if t else 0))
                    link(nc.vector.tensor_tensor(full, src.rearrange("p (h d) -> p h d", d=DIM), v_bias[:, :, :],
                                                 ALU.add))
                    link(nc.vector.tensor_copy(v_parts[:, t, :, DIM:2 * DIM], full))
                    nc.vector.tensor_tensor(v_parts[:, t, :, 0:DIM], full, v_parts[:, t, :, DIM:2 * DIM],
                                            ALU.subtract).then_inc(work_done, 1)

                def qk_lo(h, half):
                    src = ready(("qk", h, half))
                    dve.wait_ge(hi_done, i * HIS + HI_AT["qk", h, half] + 1)
                    cols = slice(half * HALF, (half + 1) * HALF)
                    nc.vector.scalar_tensor_tensor(k_lo_hi[0:DIM, h % 2, cols], src[DIM:P, :], qk_bias[DIM:P, h:h + 1],
                                                   k_lo_hi[DIM:P, h % 2, cols].bitcast(f32), ALU.add, ALU.subtract)
                    nc.vector.scalar_tensor_tensor(q_shift[DIM:P, h % 2, cols], src[0:DIM, :], qk_bias[0:DIM, h:h + 1],
                                                   q_hi_hi[0:DIM, h % 2, cols].bitcast(f32), ALU.add,
                                                   ALU.subtract).then_inc(work_done, 1)

                def row_max_part(u, q_tile, k_half):
                    src = ready(("row_max", u, q_tile, k_half))
                    if (q_tile, k_half) == (0, 0):
                        dve.wait_ge(max_ready, i * UNITS + max(u - 1, 0))
                    ins = nc.vector.reduce_max(max_parts[:, u % 2, q_tile, k_half:k_half + 1], src, AX.X)
                    ins.then_inc(work_done, 1)
                    if (q_tile, k_half) == (Q_TILES - 1, 1):
                        dve.wait_ge(work_done, i * WORKS + WORK_AT["row_max", u, q_tile, k_half] + 1)
                        nc.vector.tensor_reduce(row_max[:, u % 2, :], max_parts[:, u % 2, :, :], AX.X,
                                                ALU.max).then_inc(max_ready, 1)

                def shift_rows(u):
                    h, half = divmod(u, HALVES)
                    src = ready(("shift", u))
                    nc.vector.tensor_tensor(
                        q_shift[0:Q_TILES, h % 2, half * HALF:(half + 1) * HALF].rearrange("r (t q) -> r t q", q=P),
                        src[0:Q_TILES, 0:P].rearrange("r (o q) -> r o q", o=1).broadcast_to([Q_TILES, Q_TILES, P]),
                        minus_block[:, :, :], ALU.mult).then_inc(work_done, 1)

                def project_add(t):
                    src = ready(("project", t))
                    dve.wait_ge(y_biased, i * TOKEN_TILES + t + 1)
                    y = y_tile[:, t % Y_SLOTS, :]
                    nc.vector.tensor_tensor(y, src, y, ALU.add).then_inc(work_done, 1)

                def step_lo(s):
                    dve.wait_ge(p_full_ready, i * STEPS + s + 1)
                    dve.wait_ge(p_hi_ready, i * STEPS + s + 1)
                    dve.wait_ge(pv_done, i * STEPS + max(s + 1 - P_SLOTS, 0))
                    nc.vector.tensor_tensor(p_lo[:, s % P_SLOTS, :, :], p_full[:, s % 2, :, :],
                                            p_hi[:, s % P_SLOTS, :, :], ALU.subtract).then_inc(p_lo_ready, 1)

                def unit_output(u):
                    h, half = divmod(u, HALVES)
                    dve.wait_ge(o_lo_ready, i * UNITS + u + 1)
                    dve.wait_ge(o_ready, i * UNITS + u)
                    for bank in range(2):
                        tiles = pv[:, bank, 0:2 * PV_W].rearrange("p (t e) -> p t e", e=PV_W)
                        qs = slice(2 * bank, 2 * bank + 2)
                        nc.vector.reciprocal(inv_sum[:, qs], tiles[:, :, 2 * DIM])
                        last = nc.vector.tensor_tensor(o_sum[:, qs, :], tiles[:, :, DIM:2 * DIM], o_lo[:, qs, :], ALU.add)
                    last.then_inc(o_free, 1)
                    dve.wait_ge(o_free, i * UNITS + u + 1)
                    nc.vector.tensor_tensor(
                        o_heads[:, half * Q_TILES:(half + 1) * Q_TILES, h * DIM:(h + 1) * DIM], o_sum[:, :, :],
                        inv_sum[:, :].rearrange("p (t o) -> p t o", o=1).broadcast_to([P, Q_TILES, DIM]),
                        ALU.mult).then_inc(o_ready, 1)

                kinds = {"v": v_split, "qk": qk_lo, "row_max": row_max_part, "shift": shift_rows,
                         "project": project_add}
                for w in works_before_attention():
                    transposed_lo(w) if w[0] == "x_transpose" else kinds[w[0]](*w[1:])
                for s in range(FIRST_SLOT, LAST_SLOT + 1):
                    if s >= 5 and s % STEPS_PER_UNIT == 1:
                        unit_output((s - 5) // STEPS_PER_UNIT)
                    for w in works_of_slot(s):
                        kinds[w[0]](*w[1:])
                    if 0 <= s < STEPS:
                        step_lo(s)
                for w in works_after_attention():
                    transposed_lo(w) if w[0] == "o_transpose" else kinds[w[0]](*w[1:])
                assert linked[0] == V_LINKS * TOKEN_TILES


_INPUTS = ["x", "L0_conv_w_qkv", "L0_conv_b_qkv", "L0_conv_w_out", "L0_conv_b_out"]


def kernel(**inputs):
    import numpy as np
    import concourse.bacc as bacc
    from concourse.bass_utils import run_bass_kernel_spmd

    nc = bacc.Bacc("TRN2", target_bir_lowering=False, num_devices=1)
    arrays, args = {}, []
    for name in _INPUTS:
        a = np.ascontiguousarray(inputs[name])
        arrays[f"in_{name}"] = a
        args.append(nc.dram_tensor(f"in_{name}", a.shape, mybir.dt.from_np(a.dtype), kind="ExternalInput").ap())
    result = nc.dram_tensor("result", (BATCH, HEIGHT, WIDTH, CH), mybir.dt.float32, kind="ExternalOutput").ap()
    attention_block(nc, *args, result)
    done = run_bass_kernel_spmd(nc, [arrays], core_ids=[0])
    return done.results[0]["result"]
```

```python
from contextlib import ExitStack

import concourse.bass as bass
from concourse import mybir

P = 128
BATCH, HEIGHT, WIDTH, CH = 16, 32, 32, 512
TOKENS = HEIGHT * WIDTH
HEADS, DIM = 8, 64
SCALE = DIM ** -0.5
QKV = 3 * DIM
TOKEN_TILES = TOKENS // P
CH_TILES = CH // P
HALF = 512
HALVES = TOKENS // HALF
Q_TILES = HALF // P
UNITS = HEADS * HALVES
STEPS_PER_UNIT = 4
STEPS = UNITS * STEPS_PER_UNIT
KEYS_PER_STEP = TOKENS // STEPS_PER_UNIT // P
X_SLOTS, Y_SLOTS, P_SLOTS = 4, 4, 3
SCORE_BANKS = 3
V_WIDTH = 2 * DIM + 2
PV_W = 2 * DIM + 1
FIRST_SLOT = -5
LAST_SLOT = STEPS + 1



def max_tiles_of_slot(s, late=False):
    unit, slot = divmod(s + 5, STEPS_PER_UNIT)
    if not 0 <= unit < UNITS:
        return []
    early, later = (((0, 1), (2,)), ((3, 4), ()), ((5, 6), ()), ((7,), ()))[slot]
    return [("row_max", unit, n // 2, n % 2) for n in (later if late else early)]


def shift_unit_of_slot(s):
    unit, rest = divmod(s + 2, Q_TILES)
    return unit if rest == 0 and 0 <= unit < UNITS else None


TERMS = 3 * CH_TILES


def fills_of_slot(s):
    v_slots = {-5: (1, 2), -4: (3,), -3: (4,), -2: (5, 6), -1: (7,)}
    parts = [(("v", t), 0, TERMS) for t in v_slots.get(s, ())]
    for h in range(1, HEADS):
        begin = 8 * (h - 1)
        if begin - 4 <= s < begin - 1:
            n = s - (begin - 4)
            parts.append((("qk", h, 0), 4 * n, 4 * n + 4))
        if begin <= s < begin + 2:
            n = s - begin
            parts.append((("qk", h, 1), 6 * n, 6 * n + 6))
    tail = {STEPS - 1: (("o_transpose", 0), ("o_transpose", 1)),
            STEPS: (("project", 0), ("o_transpose", 2)),
            STEPS + 1: (("project", 1), ("o_transpose", 3))}
    return parts + [(w, 0, TERMS) for w in tail.get(s, ())]


def consumed_in_slot(s):
    tiles = []
    for (w, _, last) in fills_of_slot(s):
        if last == TERMS and not (w[0] == "qk" and w[2] == 0):
            tiles.append(w)
    late = [w for w, _, last in fills_of_slot(s - 1) if last == TERMS and w[0] == "qk" and w[2] == 0]
    return late + tiles


BEFORE = ([("x_transpose", t) for t in range(6)] + [("qk", 0, 0), ("x_transpose", 6), ("x_transpose", 7),
                                                    ("v", 0), ("qk", 0, 1)])
AFTER = [("project", 2), ("project", 3), ("o_transpose", 4), ("o_transpose", 5), ("project", 4),
         ("o_transpose", 6), ("project", 5), ("o_transpose", 7), ("project", 6), ("project", 7)]
SLOTS = range(FIRST_SLOT, LAST_SLOT + 1)

MAX_ORDER = []
for _s in SLOTS:
    MAX_ORDER += max_tiles_of_slot(_s) + max_tiles_of_slot(_s, late=True)
    if shift_unit_of_slot(_s) is not None:
        MAX_ORDER.append(("shift", shift_unit_of_slot(_s)))
MAX_AT = {w: n for n, w in enumerate(MAX_ORDER)}
MAXES = len(MAX_ORDER)

FILL_ORDER = BEFORE + [w for _s in SLOTS for w, _, last in fills_of_slot(_s) if last == TERMS] + AFTER
FILL_AT = {w: n for n, w in enumerate(FILL_ORDER)}
FILLS = len(FILL_ORDER)
assert FILL_ORDER == BEFORE + [w for _s in SLOTS for w in consumed_in_slot(_s)] + AFTER
HI_ORDER = [w for w in FILL_ORDER if w[0] in ("x_transpose", "qk", "o_transpose")]
HI_AT = {w: n for n, w in enumerate(HI_ORDER)}
HIS = len(HI_ORDER)


def fill_banks():
    banks, after = {}, 0
    for n, w in enumerate(FILL_ORDER):
        if w[0] in ("o_transpose", "project"):
            banks[w] = (3, 4, 5)[after % 3]
            after += 1
        elif w[0] == "qk" and w[1] > 0:
            banks[w] = 3
        elif w[0] == "v":
            banks[w] = 6 + w[1] % 2
        else:
            banks[w] = (3, 6, 7)[n % 3]
    return banks


FILL_BANK = fill_banks()


def last_in_bank(w):
    before = [u for u in FILL_ORDER[:FILL_AT[w]] if FILL_BANK[u] == FILL_BANK[w]]
    return before[-1] if before else None


POOL_STEPS = (1, 2, 3, 5, 6, 7)


def on_pool(s):
    return s % (HALVES * STEPS_PER_UNIT) in POOL_STEPS


def low_parts(s):
    return sum(on_pool(t) == on_pool(s) for t in range(s + 1))


LOW_PARTS = {who: sum(on_pool(t) == who for t in range(STEPS)) for who in (False, True)}


def signals(batch, per_batch, n):
    return batch * per_batch + n


def signals_led(batch, per_batch, n):
    return batch * per_batch + n + 1


def attention_block(nc: bass.Bass, x, w_qkv, b_qkv, w_out, b_out, out):
    f32, f32r, f16 = mybir.dt.float32, mybir.dt.float32r, mybir.dt.float16
    ALU, ACT, AX = mybir.AluOpType, mybir.ActivationFunctionType, mybir.AxisListType
    assert MAXES % 2 == 0

    x_tok = x.rearrange("b h w c -> b (h w) c")
    out_tok = out.rearrange("b h w c -> b (h w) c")

    with ExitStack() as ctx:
        def sb(name, shape, dt):
            return ctx.enter_context(nc.sbuf_tensor(name, shape, dt))

        def sem(name):
            return ctx.enter_context(nc.semaphore(name))

        wqkv_hi = sb("wqkv_hi", [P, CH_TILES, HEADS * QKV], f32r)
        wqkv_lo = sb("wqkv_lo", [P, CH_TILES, HEADS * QKV], f32r)
        wout_hi = sb("wout_hi", [P, CH_TILES, CH], f32r)
        wout_lo = sb("wout_lo", [P, CH_TILES, CH], f32r)
        xT_hi = sb("xT_hi", [P, CH_TILES, TOKENS], f32r)
        xT_lo = sb("xT_lo", [P, CH_TILES, TOKENS], f32r)
        x_in = sb("x_in", [P, X_SLOTS, CH], f32)
        o_heads = sb("o_heads", [P, TOKEN_TILES, CH], f32)
        v_parts = sb("v_parts", [P, TOKEN_TILES, HEADS, V_WIDTH], f16)
        v_full = sb("v_full", [P, CH], f32)
        k_lo_hi = sb("k_lo_hi", [P, 2, TOKENS], f32r)
        k_shift = sb("k_shift", [P, 2, TOKENS], f32r)
        q_hi_hi = sb("q_hi_hi", [P, 2, TOKENS], f32r)
        q_shift = sb("q_shift", [P, 2, TOKENS], f32r)
        p_full = sb("p_full", [P, 2, KEYS_PER_STEP, HALF], f32)
        p_hi = sb("p_hi", [P, P_SLOTS, KEYS_PER_STEP, HALF], f16)
        p_lo = sb("p_lo", [P, P_SLOTS, KEYS_PER_STEP, HALF], f16)
        y_tile = sb("y_tile", [P, Y_SLOTS, CH], f32)
        identity = sb("identity", [P, P], f32)
        qk_bias = sb("qk_bias", [P, HEADS], f32)
        v_bias = sb("v_bias", [P, HEADS, DIM], f32)
        out_bias = sb("out_bias", [P, CH], f32)
        minus_block = sb("minus_block", [Q_TILES, Q_TILES, P], f32)
        max_parts = sb("max_parts", [P, 2, Q_TILES, 2], f32)
        row_max = sb("row_max", [P, 2, Q_TILES], f32)
        o_lo = sb("o_lo", [P, Q_TILES, DIM], f32)
        o_sum = sb("o_sum", [P, Q_TILES, DIM], f32)
        inv_sum = sb("inv_sum", [P, Q_TILES], f32)
        stage = o_heads

        psum = ctx.enter_context(nc.psum_tensor("psum", [P, 8, HALF], f32))
        pv = psum[:, 6:8, :]

        def max_bank(w):
            return psum[:, 4 + MAX_AT[w] % 2, :]

        def fill_bank(w):
            return psum[:, FILL_BANK[w], :]

        def score_bank(tile):
            return psum[:, tile % SCORE_BANKS, :]

        def pv_columns(first, last):
            return pv[:, :, 0:2 * PV_W].rearrange("p b (t e) -> p b t e", e=PV_W)[:, :, :, first:last]

        weights_in = sem("weights_in")
        consts_in = sem("consts_in")
        w_hi_done = sem("w_hi_done")
        w_lo_done = sem("w_lo_done")
        consts_ready = sem("consts_ready")
        fills = sem("fills")
        x_loaded = [sem(f"x_loaded{k}") for k in range(X_SLOTS)]
        y_loaded = [sem(f"y_loaded{k}") for k in range(Y_SLOTS)]
        y_stored = [sem(f"y_stored{k}") for k in range(Y_SLOTS)]
        y_biased = sem("y_biased")
        fill_ready = sem("fill_ready")
        fill_done = sem("fill_done")
        hi_done = sem("hi_done")
        max_tile_ready = sem("max_tile_ready")
        max_tile_done = sem("max_tile_done")
        k_shift_ready = [sem(f"k_shift_ready{k}") for k in range(HALVES)]
        q_hi_hi_ready = [sem(f"q_hi_hi_ready{k}") for k in range(HALVES)]
        scores_ready = sem("scores_ready")
        exp_done = sem("exp_done")
        p_lo_ready = [sem(f"p_lo_ready{k}") for k in range(2)]
        DVE, POOL = False, True
        pv_done = sem("pv_done")
        max_ready = sem("max_ready")
        o_lo_ready = sem("o_lo_ready")
        o_free = sem("o_free")
        o_ready = sem("o_ready")
        dve_chain = sem("dve_chain")

        block = ctx.enter_context(nc.Block())

        def score_tiles(step):
            return [KEYS_PER_STEP * step + n for n in range(KEYS_PER_STEP)]

        def key_tile(step, n):
            return KEYS_PER_STEP * (step % STEPS_PER_UNIT) + n

        @block.sync
        def _(sp):
            for k in range(Y_SLOTS):
                sp.sem_inc(y_stored[k])
            w_view = w_qkv.rearrange("(c p) n -> p c n", p=P)
            wo_view = w_out.rearrange("(c p) n -> p c n", p=P)
            for c in range(CH_TILES):
                for n in range(2):
                    sp.dma_start(stage[:, 2 * c + n, :], w_view[:, c, n * HALF:(n + 1) * HALF]).then_inc(weights_in, 16)
            with nc.allow_non_contiguous_dma(reason="biases, once"):
                sp.dma_start(qk_bias[:, :], b_qkv.rearrange("(h e) -> e h", e=QKV)[0:P, :]).then_inc(consts_in, 16)
            sp.dma_start(v_bias[:, :, :],
                         b_qkv.rearrange("(o h e) -> o h e", o=1, e=QKV)[:, :, 2 * DIM:QKV].broadcast_to([P, HEADS, DIM])).then_inc(consts_in, 16)
            sp.dma_start(out_bias[:, :], b_out.rearrange("(o n) -> o n", o=1).broadcast_to([P, CH])).then_inc(consts_in, 16)
            for t in range(X_SLOTS):
                sp.dma_start(x_in[:, t, :], x_tok[0, t * P:(t + 1) * P, :]).then_inc(x_loaded[t], 16)
            sp.wait_ge(w_lo_done, 8)
            for c in range(CH_TILES):
                sp.dma_start(stage[:, c, :], w_view[:, c, 2 * HALF:3 * HALF]).then_inc(weights_in, 16)
                sp.dma_start(stage[:, 4 + c, :], wo_view[:, c, :]).then_inc(weights_in, 16)

            def batch(i, last):
                def copy_hi(h):
                    for half in range(HALVES):
                        cols = slice(half * HALF, (half + 1) * HALF)
                        sp.wait_ge(hi_done, signals(i, HIS, HI_AT["qk", h, half] + 1))
                        sp.dma_start(k_shift[DIM:P, h % 2, cols].bitcast(f32),
                                     k_lo_hi[DIM:P, h % 2, cols].bitcast(f32)).then_inc(k_shift_ready[half], 16)
                        sp.dma_start(q_hi_hi[DIM:P, h % 2, cols].bitcast(f32),
                                     q_hi_hi[0:DIM, h % 2, cols].bitcast(f32)).then_inc(q_hi_hi_ready[half], 16)

                def y_load(t):
                    sp.dma_start(y_tile[:, t % Y_SLOTS, :], x_tok[i, t * P:(t + 1) * P, :]).then_inc(y_loaded[t % Y_SLOTS], 16)

                for k in range(Y_SLOTS):
                    sp.wait_ge(y_stored[k], signals_led(i, 32, 0))
                for t in range(X_SLOTS, TOKEN_TILES):
                    sp.wait_ge(fill_ready, signals(i, FILLS, FILL_AT["x_transpose", t - X_SLOTS] + 1))
                    sp.dma_start(x_in[:, t % X_SLOTS, :], x_tok[i, t * P:(t + 1) * P, :]).then_inc(x_loaded[t % X_SLOTS], 16)
                copy_hi(0)
                for t in range(Y_SLOTS):
                    y_load(t)
                if not last:
                    for t in range(X_SLOTS):
                        sp.wait_ge(fill_ready, signals(i, FILLS, FILL_AT["x_transpose", t + X_SLOTS] + 1))
                        sp.dma_start(x_in[:, t, :], x_tok[i + 1, t * P:(t + 1) * P, :]).then_inc(x_loaded[t], 16)
                for h in range(1, HEADS):
                    copy_hi(h)
                for t in range(TOKEN_TILES):
                    sp.wait_ge(fill_done, signals_led(i, FILLS, FILL_AT["project", t] + 1))
                    sp.dma_start(out_tok[i, t * P:(t + 1) * P, :], y_tile[:, t % Y_SLOTS, :]).then_inc(y_stored[t % Y_SLOTS], 16)
                    if t + Y_SLOTS < TOKEN_TILES:
                        sp.wait_ge(y_stored[t % Y_SLOTS], signals_led(i, 32, 16))
                        y_load(t + Y_SLOTS)

            with sp.Fori(0, BATCH - 1) as i:
                batch(i, False)
            batch(BATCH - 1, True)
            for k in range(Y_SLOTS):
                sp.wait_ge(y_stored[k], signals_led(BATCH, 32, 0))

        @block.gpsimd
        def _(pool):
            nc.gpsimd.memset(identity[:, :], 0.0).then_inc(consts_ready, 1)
            nc.gpsimd.memset(minus_block[:, :, :], 0.0).then_inc(consts_ready, 1)
            pool.wait_ge(consts_ready, 2)
            nc.gpsimd.affine_select(out=identity[:, :], in_=identity[:, :], compare_op=ALU.not_equal, fill=1.0,
                                    base=0, pattern=[[-1, P]], channel_multiplier=1).then_inc(consts_ready, 1)
            nc.gpsimd.affine_select(out=minus_block[:, :, :], in_=minus_block[:, :, :], compare_op=ALU.not_equal,
                                    fill=-1.0, base=0, pattern=[[-1, Q_TILES], [0, P]],
                                    channel_multiplier=1).then_inc(consts_ready, 1)
            pool.wait_ge(consts_in, 48)
            pool.sem_inc(p_lo_ready[POOL])
            pool.sem_inc(o_ready)
            with pool.Fori(0, BATCH) as i:
                def step_lo(s):
                    pool.wait_ge(exp_done, signals_led(i, KEYS_PER_STEP * STEPS, score_tiles(s)[-1] + 1))
                    pool.wait_ge(pv_done, signals_led(i, STEPS, max(s + 1 - P_SLOTS, 0)))
                    nc.gpsimd.tensor_tensor(p_lo[:, s % P_SLOTS, :, :], p_full[:, s % 2, :, :],
                                            p_hi[:, s % P_SLOTS, :, :], ALU.subtract).then_inc(p_lo_ready[POOL], 1)

                def normalise(u):
                    h, half = divmod(u, HALVES)
                    pool.wait_ge(o_free, signals_led(i, UNITS, u + 1))
                    nc.gpsimd.tensor_tensor(
                        o_heads[:, half * Q_TILES:(half + 1) * Q_TILES, h * DIM:(h + 1) * DIM], o_sum[:, :, :],
                        inv_sum[:, :].rearrange("p (t o) -> p t o", o=1).broadcast_to([P, Q_TILES, DIM]),
                        ALU.mult).then_inc(o_ready, 1)

                def y_bias(t):
                    pool.wait_ge(y_loaded[t % Y_SLOTS], signals(i, 32, 16 * (t // Y_SLOTS + 1)))
                    nc.gpsimd.tensor_tensor(y_tile[:, t % Y_SLOTS, :], y_tile[:, t % Y_SLOTS, :], out_bias[:, :],
                                            ALU.add).then_inc(y_biased, 1)

                for s in range(0, LAST_SLOT + 1):
                    if s >= 5 and s % STEPS_PER_UNIT == 1:
                        normalise((s - 5) // STEPS_PER_UNIT)
                    if s < STEPS and on_pool(s):
                        step_lo(s)
                    if s % STEPS_PER_UNIT == 2 and s // STEPS_PER_UNIT < Y_SLOTS:
                        y_bias(s // STEPS_PER_UNIT)
                for t in range(Y_SLOTS, TOKEN_TILES):
                    y_bias(t)

        @block.tensor
        def _(pe):
            pe.wait_ge(consts_ready, 4)
            pe.wait_ge(w_lo_done, 16)
            pe.wait_ge(fills, 1)

            pe.sem_inc(pv_done)

            with pe.Fori(0, BATCH) as i:
                def claim_fill(w):
                    before = last_in_bank(w)
                    pe.wait_ge(fill_done, signals_led(i, FILLS, 0 if before is None else FILL_AT[before] + 1))
                    if before is None and FILL_BANK[w] >= 6:
                        pe.wait_ge(o_free, signals_led(i, UNITS, 0))
                    if before is None and FILL_BANK[w] in (4, 5):
                        pe.wait_ge(max_tile_done, signals_led(i, MAXES, MAXES))
                    return fill_bank(w)

                def claim_max(w):
                    n = MAX_AT[w]
                    if n < 2:
                        pe.wait_ge(fill_done, signals_led(i, FILLS, 0))
                    else:
                        pe.wait_ge(max_tile_done, signals_led(i, MAXES, n - 1))
                    return max_bank(w)

                def three_terms(a_hi, a_lo, b_hi, b_lo):
                    return [pair for c in range(CH_TILES) for pair in
                            ((a_hi(c), b_hi(c)), (a_hi(c), b_lo(c)), (a_lo(c), b_hi(c)))]

                def v_cols(w):
                    return lambda c: w[:, c, :].rearrange("p (h e) -> p h e", e=QKV)[:, :, 2 * DIM:QKV]

                def terms_of(w):
                    if w[0] == "qk":
                        toks = slice(w[2] * HALF, (w[2] + 1) * HALF)
                        cols = slice(w[1] * QKV, w[1] * QKV + 2 * DIM)
                        return three_terms(lambda c: wqkv_hi[:, c, cols], lambda c: wqkv_lo[:, c, cols],
                                           lambda c: xT_hi[:, c, toks], lambda c: xT_lo[:, c, toks])
                    toks = slice(w[1] * P, (w[1] + 1) * P)
                    left = lambda c: xT_hi[:, c, toks], lambda c: xT_lo[:, c, toks]
                    if w[0] == "v":
                        return three_terms(*left, v_cols(wqkv_hi), v_cols(wqkv_lo))
                    return three_terms(*left, lambda c: wout_hi[:, c, :], lambda c: wout_lo[:, c, :])

                def projection(w, first, last):
                    if first == 0:
                        claim_fill(w)
                        source = {"qk": lambda: ("x_transpose", 4 * w[2] + 3), "v": lambda: ("x_transpose", w[1]),
                                  "project": lambda: ("o_transpose", w[1])}[w[0]]()
                        pe.wait_ge(fill_done, signals_led(i, FILLS, FILL_AT[source] + 1))
                    for n, (a, b) in list(enumerate(terms_of(w)))[first:last]:
                        matmul = nc.tensor.matmul(fill_bank(w), a, b, start=n == 0, stop=n == TERMS - 1)
                    if last == TERMS:
                        matmul.then_inc(fill_ready, 1)

                def transpose(w):
                    dst, t = claim_fill(w), w[1]
                    if w[0] == "x_transpose":
                        pe.wait_ge(x_loaded[t % X_SLOTS], signals(i, 32, 16 * (t // X_SLOTS + 1)))
                        src = x_in[:, t % X_SLOTS, :]
                    else:
                        pe.wait_ge(o_ready, signals_led(i, UNITS, UNITS - 1 + t // Q_TILES))
                        src = o_heads[:, t, :]
                    for c in range(CH_TILES):
                        last = nc.tensor.transpose(dst[:, c * P:(c + 1) * P], src[:, c * P:(c + 1) * P], identity[:, :])
                    last.then_inc(fill_ready, 1)

                def fill(w, first=0, last=TERMS):
                    if w[0] in ("x_transpose", "o_transpose"):
                        transpose(w)
                    else:
                        projection(w, first, last)

                def row_max_tile(w):
                    _, u, q_tile, k_half = w
                    h, half = divmod(u, HALVES)
                    dst = claim_max(w)
                    pe.wait_ge(fill_done, signals_led(i, FILLS, FILL_AT["qk", h, 1] + 1))
                    pe.wait_ge(q_hi_hi_ready[half], signals(i, HEADS * 16, (h + 1) * 16))
                    q0 = half * HALF + q_tile * P
                    nc.tensor.matmul(dst, q_hi_hi[:, h % 2, q0:q0 + P],
                                     k_lo_hi[:, h % 2, k_half * HALF:(k_half + 1) * HALF],
                                     start=True, stop=True).then_inc(max_tile_ready, 1)

                def shift_tile(u):
                    dst = claim_max(("shift", u))
                    pe.wait_ge(max_ready, signals_led(i, UNITS, u + 1))
                    nc.tensor.transpose(dst[0:Q_TILES, 0:P], row_max[:, u % 2, :],
                                        identity[:, :]).then_inc(max_tile_ready, 1)

                def step_scores(s):
                    u = s // STEPS_PER_UNIT
                    h, half = divmod(u, HALVES)
                    if s % STEPS_PER_UNIT == 0:
                        pe.wait_ge(max_tile_done, signals_led(i, MAXES, MAX_AT["shift", u] + 1))
                        if half == 0:
                            for k in range(HALVES):
                                pe.wait_ge(k_shift_ready[k], signals(i, HEADS * 16, (h + 1) * 16))
                    cols = slice(half * HALF, (half + 1) * HALF)
                    for n, tile in enumerate(score_tiles(s)):
                        pe.wait_ge(exp_done, signals_led(i, KEYS_PER_STEP * STEPS, max(tile + 1 - SCORE_BANKS, 0)))
                        keys = slice(key_tile(s, n) * P, (key_tile(s, n) + 1) * P)
                        nc.tensor.matmul(score_bank(tile), k_lo_hi[:, h % 2, keys], q_hi_hi[:, h % 2, cols],
                                         start=True, stop=False)
                        nc.tensor.matmul(score_bank(tile), k_shift[:, h % 2, keys], q_shift[:, h % 2, cols],
                                         start=False, stop=True).then_inc(scores_ready, 1)

                def step_pv(s):
                    u = s // STEPS_PER_UNIT
                    h = u // HALVES
                    if s == 0:
                        pe.wait_ge(fill_done, signals_led(i, FILLS, FILL_AT["v", TOKEN_TILES - 1] + 1))
                    if s % STEPS_PER_UNIT == 0:
                        pe.wait_ge(o_free, signals_led(i, UNITS, u))
                    pe.wait_ge(exp_done, signals_led(i, KEYS_PER_STEP * STEPS, score_tiles(s)[-1] + 1))
                    pe.wait_ge(p_lo_ready[on_pool(s)], signals_led(i, LOW_PARTS[on_pool(s)], low_parts(s)))
                    for n in range(KEYS_PER_STEP):
                        kt = key_tile(s, n)
                        for qt in range(Q_TILES):
                            bank, col = qt // 2, (qt % 2) * PV_W
                            qs = slice(qt * P, (qt + 1) * P)
                            nc.tensor.matmul(pv[:, bank, col:col + PV_W], p_hi[:, s % P_SLOTS, n, qs],
                                             v_parts[:, kt, h, 0:PV_W], start=kt == 0 and qt % 2 == 0,
                                             stop=False, skip_group_check=True)
                            last = nc.tensor.matmul(pv[:, bank, col + DIM:col + PV_W], p_lo[:, s % P_SLOTS, n, qs],
                                                    v_parts[:, kt, h, DIM:PV_W], start=False,
                                                    stop=kt == TOKEN_TILES - 1, skip_group_check=True)
                    last.then_inc(pv_done, 1)

                for w in BEFORE:
                    fill(w)
                for s in SLOTS:
                    if s < 0 or s >= STEPS:
                        if s == STEPS:
                            step_pv(s - 1)
                        for part in fills_of_slot(s):
                            fill(*part)
                    for w in max_tiles_of_slot(s):
                        row_max_tile(w)
                    fills_after_scores = s % 8 == 0
                    if 0 <= s < STEPS and not fills_after_scores:
                        for part in fills_of_slot(s):
                            fill(*part)
                    if 0 <= s + 1 < STEPS:
                        step_scores(s + 1)
                    if 0 <= s < STEPS and fills_after_scores:
                        for part in fills_of_slot(s):
                            fill(*part)
                    for w in max_tiles_of_slot(s, late=True):
                        row_max_tile(w)
                    if shift_unit_of_slot(s) is not None:
                        shift_tile(shift_unit_of_slot(s))
                    if 1 <= s < STEPS:
                        step_pv(s - 1)
                for w in AFTER:
                    fill(w)

        @block.scalar
        def _(act):
            for n in range(2 * TOKEN_TILES):
                rnd, slot = divmod(n, 8)
                if slot == 0:
                    act.wait_ge(weights_in, 128 * (rnd + 1))
                if rnd == 0:
                    c, part = divmod(slot, 2)
                    dst = wqkv_hi[:, c, part * HALF:(part + 1) * HALF]
                elif slot < CH_TILES:
                    dst = wqkv_hi[:, slot, 2 * HALF:3 * HALF]
                else:
                    dst = wout_hi[:, slot - CH_TILES, :]
                nc.scalar.copy(dst, stage[:, slot, :]).then_inc(w_hi_done, 1)
            act.wait_ge(consts_in, 48)
            act.sem_inc(exp_done)

            with act.Fori(0, BATCH) as i:
                def transposed_hi(w):
                    t = w[1]
                    act.wait_ge(fill_ready, signals(i, FILLS, FILL_AT[w] + 1))
                    nc.scalar.copy(xT_hi[:, :, t * P:(t + 1) * P],
                                   fill_bank(w).rearrange("p (c k) -> p c k", c=CH_TILES)).then_inc(hi_done, 1)

                def qk_hi(w):
                    _, h, half = w
                    cols = slice(half * HALF, (half + 1) * HALF)
                    act.wait_ge(fill_ready, signals(i, FILLS, FILL_AT[w] + 1))
                    q, k = fill_bank(w)[0:DIM, :], fill_bank(w)[DIM:P, :]
                    nc.scalar.activation(q_hi_hi[0:DIM, h % 2, cols], q, ACT.Identity, bias=qk_bias[0:DIM, h:h + 1])
                    nc.scalar.activation(k_lo_hi[DIM:P, h % 2, cols], k, ACT.Identity,
                                         bias=qk_bias[DIM:P, h:h + 1]).then_inc(hi_done, 1)

                def take_hi(w):
                    if w[0] == "qk":
                        qk_hi(w)
                    elif w[0] in ("x_transpose", "o_transpose"):
                        transposed_hi(w)

                def exp_tile(s, n):
                    tile = score_tiles(s)[n]
                    act.wait_ge(scores_ready, signals(i, KEYS_PER_STEP * STEPS, tile + 1))
                    if n == 0:
                        if s < 2:
                            for who in (False, True):
                                act.wait_ge(p_lo_ready[who], signals_led(i, LOW_PARTS[who], 0))
                        else:
                            act.wait_ge(p_lo_ready[on_pool(s - 2)],
                                        signals_led(i, LOW_PARTS[on_pool(s - 2)], low_parts(s - 2)))
                        act.wait_ge(pv_done, signals_led(i, STEPS, max(s + 1 - P_SLOTS, 0)))
                    nc.scalar.activation(p_full[:, s % 2, n, :], score_bank(tile), ACT.Exp, scale=SCALE)
                    nc.scalar.activation(p_hi[:, s % P_SLOTS, n, :], score_bank(tile), ACT.Exp,
                                         scale=SCALE).then_inc(exp_done, 1)

                def unit_lo(u):
                    act.wait_ge(pv_done, signals_led(i, STEPS, STEPS_PER_UNIT * (u + 1)))
                    act.wait_ge(o_free, signals_led(i, UNITS, u))
                    nc.scalar.copy(o_lo[:, :, :].rearrange("p (b t) d -> p b t d", b=2),
                                   pv_columns(0, DIM)).then_inc(o_lo_ready, 1)

                for w in BEFORE:
                    take_hi(w)
                for s in SLOTS:
                    if 0 <= s < STEPS:
                        exp_tile(s, 0)
                    if s >= 5 and s % STEPS_PER_UNIT == 1:
                        unit_lo((s - 5) // STEPS_PER_UNIT)
                    if 0 <= s < STEPS:
                        exp_tile(s, 1)
                    for w in consumed_in_slot(s):
                        take_hi(w)
                for w in AFTER:
                    take_hi(w)

        @block.vector
        def _(dve):
            nc.vector.memset(k_shift[0:DIM, :, :].bitcast(f32), 0.0).then_inc(dve_chain, 1)
            nc.vector.memset(q_shift[0:DIM, :, :].bitcast(f32), 0.0)
            nc.vector.memset(v_parts[:, :, :, 2 * DIM:V_WIDTH], 1.0)
            dve.wait_ge(dve_chain, 1)
            nc.vector.memset(k_shift[0:Q_TILES, :, :].bitcast(f32), 1.0).then_inc(fills, 1)
            for n in range(2 * TOKEN_TILES):
                rnd, slot = divmod(n, 8)
                dve.wait_ge(w_hi_done, n + 1)
                if rnd == 0:
                    c, part = divmod(slot, 2)
                    where = (slice(None), c, slice(part * HALF, (part + 1) * HALF))
                    hi, lo = wqkv_hi[where], wqkv_lo[where]
                elif slot < CH_TILES:
                    where = (slice(None), slot, slice(2 * HALF, 3 * HALF))
                    hi, lo = wqkv_hi[where], wqkv_lo[where]
                else:
                    hi, lo = wout_hi[:, slot - CH_TILES, :], wout_lo[:, slot - CH_TILES, :]
                nc.vector.tensor_tensor(lo, stage[:, slot, :], hi.bitcast(f32), ALU.subtract).then_inc(w_lo_done, 1)
            dve.wait_ge(consts_in, 48)
            dve.wait_ge(consts_ready, 4)
            for led in (fill_done, max_tile_done, p_lo_ready[DVE], o_free, max_ready):
                dve.sem_inc(led)
            V_LINKS = 2
            LINKS = V_LINKS * TOKEN_TILES

            with dve.Fori(0, BATCH) as i:
                linked = [0]

                def link(ins):
                    ins.then_inc(dve_chain, 1)
                    linked[0] += 1
                    dve.wait_ge(dve_chain, i * LINKS + 1 + linked[0])

                def transposed_lo(w):
                    t = w[1]
                    dve.wait_ge(hi_done, signals(i, HIS, HI_AT[w] + 1))
                    toks = slice(t * P, (t + 1) * P)
                    nc.vector.tensor_tensor(xT_lo[:, :, toks], fill_bank(w).rearrange("p (c k) -> p c k", c=CH_TILES),
                                            xT_hi[:, :, toks].bitcast(f32), ALU.subtract).then_inc(fill_done, 1)

                def v_split(w):
                    t = w[1]
                    full = v_full[:, :].rearrange("p (h d) -> p h d", d=DIM)
                    dve.wait_ge(fill_done, signals_led(i, FILLS, FILL_AT["v", t - 1] + 1 if t else 0))
                    link(nc.vector.tensor_tensor(full, fill_bank(w).rearrange("p (h d) -> p h d", d=DIM),
                                                 v_bias[:, :, :], ALU.add))
                    link(nc.vector.tensor_copy(v_parts[:, t, :, DIM:2 * DIM], full))
                    nc.vector.tensor_tensor(v_parts[:, t, :, 0:DIM], full, v_parts[:, t, :, DIM:2 * DIM],
                                            ALU.subtract).then_inc(fill_done, 1)

                def qk_lo(w):
                    _, h, half = w
                    src = fill_bank(w)
                    dve.wait_ge(hi_done, signals(i, HIS, HI_AT[w] + 1))
                    cols = slice(half * HALF, (half + 1) * HALF)
                    nc.vector.scalar_tensor_tensor(k_lo_hi[0:DIM, h % 2, cols], src[DIM:P, :], qk_bias[DIM:P, h:h + 1],
                                                   k_lo_hi[DIM:P, h % 2, cols].bitcast(f32), ALU.add, ALU.subtract)
                    nc.vector.scalar_tensor_tensor(q_shift[DIM:P, h % 2, cols], src[0:DIM, :], qk_bias[0:DIM, h:h + 1],
                                                   q_hi_hi[0:DIM, h % 2, cols].bitcast(f32), ALU.add,
                                                   ALU.subtract).then_inc(fill_done, 1)

                def project_add(w):
                    t = w[1]
                    dve.wait_ge(y_biased, signals(i, TOKEN_TILES, t + 1))
                    y = y_tile[:, t % Y_SLOTS, :]
                    nc.vector.tensor_tensor(y, fill_bank(w), y, ALU.add).then_inc(fill_done, 1)

                def take(w):
                    dve.wait_ge(fill_ready, signals(i, FILLS, FILL_AT[w] + 1))
                    {"x_transpose": transposed_lo, "o_transpose": transposed_lo, "v": v_split, "qk": qk_lo,
                     "project": project_add}[w[0]](w)

                def row_max_part(w):
                    _, u, q_tile, k_half = w
                    dve.wait_ge(max_tile_ready, signals(i, MAXES, MAX_AT[w] + 1))
                    if (q_tile, k_half) == (0, 0):
                        dve.wait_ge(max_ready, signals_led(i, UNITS, max(u - 1, 0)))
                    nc.vector.reduce_max(max_parts[:, u % 2, q_tile, k_half:k_half + 1], max_bank(w),
                                         AX.X).then_inc(max_tile_done, 1)

                def join_max(u):
                    dve.wait_ge(max_tile_done, signals_led(i, MAXES, MAX_AT["row_max", u, Q_TILES - 1, 1] + 1))
                    nc.vector.tensor_reduce(row_max[:, u % 2, :], max_parts[:, u % 2, :, :], AX.X,
                                            ALU.max).then_inc(max_ready, 1)

                def shift_rows(u):
                    h, half = divmod(u, HALVES)
                    w = ("shift", u)
                    dve.wait_ge(max_tile_ready, signals(i, MAXES, MAX_AT[w] + 1))
                    nc.vector.tensor_tensor(
                        q_shift[0:Q_TILES, h % 2, half * HALF:(half + 1) * HALF].rearrange("r (t q) -> r t q", q=P),
                        max_bank(w)[0:Q_TILES, 0:P].rearrange("r (o q) -> r o q", o=1).broadcast_to([Q_TILES, Q_TILES, P]),
                        minus_block[:, :, :], ALU.mult).then_inc(max_tile_done, 1)

                def step_lo(s):
                    dve.wait_ge(exp_done, signals_led(i, KEYS_PER_STEP * STEPS, score_tiles(s)[-1] + 1))
                    dve.wait_ge(pv_done, signals_led(i, STEPS, max(s + 1 - P_SLOTS, 0)))
                    nc.vector.tensor_tensor(p_lo[:, s % P_SLOTS, :, :], p_full[:, s % 2, :, :],
                                            p_hi[:, s % P_SLOTS, :, :], ALU.subtract).then_inc(p_lo_ready[DVE], 1)

                def unit_output(u):
                    dve.wait_ge(o_lo_ready, signals(i, UNITS, u + 1))
                    dve.wait_ge(o_ready, signals_led(i, UNITS, u))
                    nc.vector.reciprocal(inv_sum[:, :].rearrange("p (b t o) -> p b t o", b=2, o=1),
                                         pv_columns(2 * DIM, PV_W))
                    nc.vector.tensor_tensor(o_sum[:, :, :].rearrange("p (b t) d -> p b t d", b=2),
                                            pv_columns(DIM, 2 * DIM),
                                            o_lo[:, :, :].rearrange("p (b t) d -> p b t d", b=2),
                                            ALU.add).then_inc(o_free, 1)

                for w in BEFORE:
                    take(w)
                for s in SLOTS:
                    if s < 0 or s >= STEPS:
                        if s == LAST_SLOT:
                            unit_output(UNITS - 1)
                        for w in consumed_in_slot(s):
                            take(w)
                    for w in max_tiles_of_slot(s):
                        row_max_part(w)
                        if w[2:] == (Q_TILES - 1, 1):
                            join_max(w[1])
                    if 5 <= s < STEPS and s % STEPS_PER_UNIT == 1:
                        unit_output((s - 5) // STEPS_PER_UNIT)
                    if shift_unit_of_slot(s) is not None and s % 8 == 2:
                        shift_rows(shift_unit_of_slot(s))
                    if 0 <= s < STEPS and not on_pool(s):
                        step_lo(s)
                    for w in max_tiles_of_slot(s, late=True):
                        row_max_part(w)
                    if 0 <= s < STEPS:
                        for w in consumed_in_slot(s):
                            take(w)
                    if shift_unit_of_slot(s) is not None and s % 8 != 2:
                        shift_rows(shift_unit_of_slot(s))
                for w in AFTER:
                    take(w)
                assert linked[0] == V_LINKS * TOKEN_TILES


_INPUTS = ["x", "L0_conv_w_qkv", "L0_conv_b_qkv", "L0_conv_w_out", "L0_conv_b_out"]


def kernel(**inputs):
    import numpy as np
    import concourse.bacc as bacc
    from concourse.bass_utils import run_bass_kernel_spmd

    nc = bacc.Bacc("TRN2", target_bir_lowering=False, num_devices=1)
    arrays, args = {}, []
    for name in _INPUTS:
        a = np.ascontiguousarray(inputs[name])
        arrays[f"in_{name}"] = a
        args.append(nc.dram_tensor(f"in_{name}", a.shape, mybir.dt.from_np(a.dtype), kind="ExternalInput").ap())
    result = nc.dram_tensor("result", (BATCH, HEIGHT, WIDTH, CH), mybir.dt.float32, kind="ExternalOutput").ap()
    attention_block(nc, *args, result)
    done = run_bass_kernel_spmd(nc, [arrays], core_ids=[0])
    return done.results[0]["result"]
```

```python
import math
from contextlib import ExitStack

import concourse.bass as bass
from concourse import mybir

P = 128
BATCH, HEIGHT, WIDTH, CH = 16, 32, 32, 512
TOKENS = HEIGHT * WIDTH
HEADS, DIM = 8, 64
SCALE = DIM ** -0.5
PROB_BIAS = 8 * math.log(2)
QKV = 3 * DIM
TOKEN_TILES = TOKENS // P
CH_TILES = CH // P
HALF = 512
HALVES = TOKENS // HALF
Q_TILES = HALF // P
UNITS = HEADS * HALVES
STEPS_PER_UNIT = 4
STEPS = UNITS * STEPS_PER_UNIT
STEPS_PER_HEAD = HALVES * STEPS_PER_UNIT
KEYS_PER_STEP = TOKENS // STEPS_PER_UNIT // P
X_SLOTS, Y_SLOTS, P_SLOTS = 4, 4, 3
SCORE_BANKS = 3
V_WIDTH = 2 * DIM + 2
PV_W = 2 * DIM + 1
FIRST_SLOT = -5
LAST_SLOT = STEPS + 1



MAX_TILES = (((0, 1), (2,)), ((3, 4), ()), ((5, 6), (7,)), ((), ()))
MAX_TILES_OF_UNIT = {0: (((0, 1), ()), ((2, 3), ()), ((4, 5), ()), ((6, 7), ())),
                     1: (((0, 1), ()), ((2, 3), ()), ((4, 5), (6,)), ((7,), ()))}


def max_tiles_of_slot(s, late=False):
    unit, slot = divmod(s + 5, STEPS_PER_UNIT)
    if not 0 <= unit < UNITS:
        return []
    tiles = MAX_TILES_OF_UNIT.get(unit, MAX_TILES)
    return [("row_max", unit, n // 2, n % 2) for n in tiles[slot][late]]


def shift_unit_of_slot(s):
    unit, rest = divmod(s + 2, Q_TILES)
    return unit if rest == 0 and 0 <= unit < UNITS else None


TERMS = 3 * CH_TILES

QK_PARTS = ({-5: (0, 1), -4: (1, 4), -3: (4, 8), -2: (8, TERMS)}, {0: (0, 6), 1: (6, TERMS)})
V_OF_SLOT = {-5: (4,), -4: (5,), -3: (6,), -2: (7,)}


def fills_of_slot(s):
    parts = [(("v", t), 0, TERMS) for t in V_OF_SLOT.get(s, ())]
    for h in range(1, HEADS):
        begin = STEPS_PER_HEAD * (h - 1)
        for half in range(2):
            if s - begin in QK_PARTS[half]:
                parts.append((("qk", h, half), *QK_PARTS[half][s - begin]))
    tail = {STEPS - 2: (("o_transpose", 0), ("o_transpose", 1)),
            STEPS - 1: (("project", 0), ("o_transpose", 2)),
            STEPS: (("project", 1), ("o_transpose", 3), ("project", 2))}
    return parts + [(w, 0, TERMS) for w in tail.get(s, ())]


def completed_in_slot(s):
    return [w for w, _, last in fills_of_slot(s) if last == TERMS]


def is_first_half(w):
    return w[0] == "qk" and w[2] == 0


def consumed_in_slot(s):
    return ([w for w in completed_in_slot(s - 1) if is_first_half(w)]
            + [w for w in completed_in_slot(s) if not is_first_half(w)])


def high_parts_in_slot(s):
    parts = [(w, "k") for w in completed_in_slot(s - 1) if is_first_half(w)]
    for w in completed_in_slot(s):
        parts.append((w, "q" if is_first_half(w) else "qk"))
    return parts


def named(*names):
    kinds = {"T": ("x_transpose",), "V": ("v",), "Q": ("qk", 0)}
    return [(*kinds[name[0]], int(name[1])) for name in names]


BEFORE = named("T0", "T1", "T2", "T3", "V0", "T4", "T5", "Q0", "T6", "T7", "V1", "V2", "Q1", "V3")
AFTER = [("o_transpose", 4), ("project", 3), ("o_transpose", 5), ("project", 4), ("o_transpose", 6),
         ("project", 5), ("o_transpose", 7), ("project", 6), ("project", 7)]
SLOTS = range(FIRST_SLOT, LAST_SLOT + 1)

MAX_ORDER = []
for _s in SLOTS:
    MAX_ORDER += max_tiles_of_slot(_s) + max_tiles_of_slot(_s, late=True)
    if shift_unit_of_slot(_s) is not None:
        MAX_ORDER.append(("shift", shift_unit_of_slot(_s)))
MAX_AT = {w: n for n, w in enumerate(MAX_ORDER)}
MAXES = len(MAX_ORDER)

FILL_ORDER = BEFORE + [w for _s in SLOTS for w in completed_in_slot(_s)] + AFTER
FILL_AT = {w: n for n, w in enumerate(FILL_ORDER)}
FILLS = len(FILL_ORDER)
assert FILL_ORDER == BEFORE + [w for _s in SLOTS for w in consumed_in_slot(_s)] + AFTER
HI_ORDER = [w for w in FILL_ORDER if w[0] != "project"]
HI_AT = {w: n for n, w in enumerate(HI_ORDER)}
HIS = len(HI_ORDER)


def fill_banks():
    banks, after = {}, 0
    for n, w in enumerate(FILL_ORDER):
        if w[0] in ("o_transpose", "project"):
            banks[w] = (3, 4, 5)[after % 3]
            after += 1
        elif w[0] == "qk" and w[1] > 0:
            banks[w] = 3
        elif w in BEFORE:
            banks[w] = (6, 7, 0, 1, 2, 3)[n % 6]
        else:
            banks[w] = 6 + w[1] % 2
    return banks


FILL_BANK = fill_banks()


def last_in_bank(w):
    before = [u for u in FILL_ORDER[:FILL_AT[w]] if FILL_BANK[u] == FILL_BANK[w]]
    return before[-1] if before else None


POOL_STEPS = (0, 2, 3, 4, 6, 7)
LAST_UNIT_POOL_STEPS = (STEPS - 4, STEPS - 2)


def on_pool(s):
    if s >= STEPS - STEPS_PER_UNIT:
        return s in LAST_UNIT_POOL_STEPS
    return s % STEPS_PER_HEAD in POOL_STEPS


def low_parts(s):
    return sum(on_pool(t) == on_pool(s) for t in range(s + 1))


LOW_PARTS = {who: sum(on_pool(t) == who for t in range(STEPS)) for who in (False, True)}


def signals(batch, per_batch, n):
    return batch * per_batch + n


def signals_led(batch, per_batch, n):
    return batch * per_batch + n + 1


def attention_block(nc: bass.Bass, x, w_qkv, b_qkv, w_out, b_out, out):
    f32, f32r, f16 = mybir.dt.float32, mybir.dt.float32r, mybir.dt.float16
    ALU, ACT, AX = mybir.AluOpType, mybir.ActivationFunctionType, mybir.AxisListType
    assert MAXES % 2 == 0

    x_tok = x.rearrange("b h w c -> b (h w) c")
    out_tok = out.rearrange("b h w c -> b (h w) c")

    with ExitStack() as ctx:
        def sb(name, shape, dt):
            return ctx.enter_context(nc.sbuf_tensor(name, shape, dt))

        def sem(name):
            return ctx.enter_context(nc.semaphore(name))

        wqkv_hi = sb("wqkv_hi", [P, CH_TILES, HEADS * QKV], f32r)
        wqkv_lo = sb("wqkv_lo", [P, CH_TILES, HEADS * QKV], f32r)
        wout_hi = sb("wout_hi", [P, CH_TILES, CH], f32r)
        wout_lo = sb("wout_lo", [P, CH_TILES, CH], f32r)
        xT_hi = sb("xT_hi", [P, CH_TILES, TOKENS], f32r)
        xT_lo = sb("xT_lo", [P, CH_TILES, TOKENS], f32r)
        x_in = sb("x_in", [P, X_SLOTS, CH], f32)
        o_heads = sb("o_heads", [P, TOKEN_TILES, CH], f32)
        v_parts = sb("v_parts", [P, TOKEN_TILES, HEADS, V_WIDTH], f16)
        k_lo_hi = sb("k_lo_hi", [P, 2, TOKENS], f32r)
        k_shift = sb("k_shift", [P, 2, TOKENS], f32r)
        q_hi_hi = sb("q_hi_hi", [P, 2, TOKENS], f32r)
        q_shift = sb("q_shift", [P, 2, TOKENS], f32r)
        p_full = sb("p_full", [P, 2, KEYS_PER_STEP, HALF], f32)
        p_hi = sb("p_hi", [P, P_SLOTS, KEYS_PER_STEP, HALF], f16)
        p_lo = sb("p_lo", [P, P_SLOTS, KEYS_PER_STEP, HALF], f16)
        y_tile = sb("y_tile", [P, Y_SLOTS, CH], f32)
        identity = sb("identity", [P, P], f32)
        qk_bias = sb("qk_bias", [P, HEADS], f32)
        v_bias = sb("v_bias", [P, CH_TILES], f32)
        out_bias = sb("out_bias", [P, CH], f32)
        minus_block = sb("minus_block", [Q_TILES, Q_TILES, P], f32)
        max_parts = sb("max_parts", [P, 2, Q_TILES, 2], f32)
        row_max = sb("row_max", [P, 2, Q_TILES], f32)
        o_lo = sb("o_lo", [P, Q_TILES, DIM], f32)
        o_sum = sb("o_sum", [P, Q_TILES, DIM], f32)
        prob_bias = sb("prob_bias", [P, 1], f32)
        inv_sum = sb("inv_sum", [P, Q_TILES], f32)
        stage = o_heads
        zeros = p_full[:, 0, 0, 0:P]
        bias_hi, bias_lo = k_lo_hi[:, 0, 0:CH], k_lo_hi[:, 1, 0:CH]

        psum = ctx.enter_context(nc.psum_tensor("psum", [P, 8, HALF], f32))
        pv = psum[:, 6:8, :]

        def max_bank(w):
            return psum[:, 4 + MAX_AT[w] % 2, :]

        def fill_bank(w):
            return psum[:, FILL_BANK[w], :]

        def score_bank(tile):
            return psum[:, tile % SCORE_BANKS, :]

        def pv_columns(first, last):
            return pv[:, :, 0:2 * PV_W].rearrange("p b (t e) -> p b t e", e=PV_W)[:, :, :, first:last]

        weights_in = sem("weights_in")
        consts_in = sem("consts_in")
        w_hi_done = sem("w_hi_done")
        w_lo_done = sem("w_lo_done")
        bias_product = sem("bias_product")
        bias_ready = sem("bias_ready")
        consts_ready = sem("consts_ready")
        fixed_ready = sem("fixed_ready")
        x_loaded = [sem(f"x_loaded{k}") for k in range(X_SLOTS)]
        y_loaded = [sem(f"y_loaded{k}") for k in range(Y_SLOTS)]
        y_stored = [sem(f"y_stored{k}") for k in range(Y_SLOTS)]
        y_biased = sem("y_biased")
        fill_ready = sem("fill_ready")
        fill_done = sem("fill_done")
        hi_done = sem("hi_done")
        max_tile_ready = sem("max_tile_ready")
        max_tile_done = sem("max_tile_done")
        k_shift_ready = [sem(f"k_shift_ready{k}") for k in range(HALVES)]
        q_hi_hi_ready = [sem(f"q_hi_hi_ready{k}") for k in range(HALVES)]
        scores_ready = sem("scores_ready")
        exp_done = sem("exp_done")
        p_lo_ready = [sem(f"p_lo_ready{k}") for k in range(2)]
        DVE, POOL = False, True
        pv_done = sem("pv_done")
        max_ready = sem("max_ready")
        o_lo_ready = sem("o_lo_ready")
        o_free = sem("o_free")
        o_ready = sem("o_ready")
        zeroed = sem("zeroed")

        block = ctx.enter_context(nc.Block())

        def score_tiles(step):
            return [KEYS_PER_STEP * step + n for n in range(KEYS_PER_STEP)]

        def key_tile(step, n):
            return KEYS_PER_STEP * (step % STEPS_PER_UNIT) + n

        @block.sync
        def _(sp):
            for k in range(Y_SLOTS):
                sp.sem_inc(y_stored[k])
            w_view = w_qkv.rearrange("(c p) n -> p c n", p=P)
            wo_view = w_out.rearrange("(c p) n -> p c n", p=P)
            for c in range(CH_TILES):
                for n in range(2):
                    sp.dma_start(stage[:, 2 * c + n, :], w_view[:, c, n * HALF:(n + 1) * HALF]).then_inc(weights_in, 16)
            with nc.allow_non_contiguous_dma(reason="biases, once"):
                sp.dma_start(qk_bias[:, :], b_qkv.rearrange("(h e) -> e h", e=QKV)[0:P, :]).then_inc(consts_in, 16)
                for parity in range(2):
                    sp.dma_start(v_bias[parity * DIM:(parity + 1) * DIM, :],
                                 b_qkv.rearrange("(c h e) -> h e c", h=2, e=QKV)[parity, 2 * DIM:QKV, :]).then_inc(consts_in, 16)
            sp.dma_start(out_bias[:, :], b_out.rearrange("(o n) -> o n", o=1).broadcast_to([P, CH])).then_inc(consts_in, 16)
            for t in range(X_SLOTS):
                sp.dma_start(x_in[:, t, :], x_tok[0, t * P:(t + 1) * P, :]).then_inc(x_loaded[t], 16)
            sp.wait_ge(w_lo_done, TOKEN_TILES)
            for c in range(CH_TILES):
                sp.dma_start(stage[:, c, :], w_view[:, c, 2 * HALF:3 * HALF]).then_inc(weights_in, 16)
                sp.dma_start(stage[:, CH_TILES + c, :], wo_view[:, c, :]).then_inc(weights_in, 16)

            def batch(i, last):
                def copy_hi(h):
                    for half in range(HALVES):
                        cols = slice(half * HALF, (half + 1) * HALF)
                        sp.wait_ge(hi_done, signals(i, HIS, HI_AT["qk", h, half] + 1))
                        sp.dma_start(k_shift[DIM:P, h % 2, cols].bitcast(f32),
                                     k_lo_hi[DIM:P, h % 2, cols].bitcast(f32)).then_inc(k_shift_ready[half], 16)
                        sp.dma_start(q_hi_hi[DIM:P, h % 2, cols].bitcast(f32),
                                     q_hi_hi[0:DIM, h % 2, cols].bitcast(f32)).then_inc(q_hi_hi_ready[half], 16)

                def y_load(t):
                    sp.dma_start(y_tile[:, t % Y_SLOTS, :], x_tok[i, t * P:(t + 1) * P, :]).then_inc(y_loaded[t % Y_SLOTS], 16)

                for t in range(X_SLOTS, TOKEN_TILES):
                    sp.wait_ge(fill_ready, signals(i, FILLS, FILL_AT["x_transpose", t - X_SLOTS] + 1))
                    sp.dma_start(x_in[:, t % X_SLOTS, :], x_tok[i, t * P:(t + 1) * P, :]).then_inc(x_loaded[t % X_SLOTS], 16)
                for k in range(Y_SLOTS):
                    sp.wait_ge(y_stored[k], signals_led(i, 32, 0))
                copy_hi(0)
                for t in range(Y_SLOTS):
                    y_load(t)
                if not last:
                    for t in range(X_SLOTS):
                        sp.wait_ge(fill_ready, signals(i, FILLS, FILL_AT["x_transpose", t + X_SLOTS] + 1))
                        sp.dma_start(x_in[:, t, :], x_tok[i + 1, t * P:(t + 1) * P, :]).then_inc(x_loaded[t], 16)
                for h in range(1, HEADS):
                    copy_hi(h)
                for t in range(TOKEN_TILES):
                    sp.wait_ge(fill_done, signals_led(i, FILLS, FILL_AT["project", t] + 1))
                    sp.dma_start(out_tok[i, t * P:(t + 1) * P, :], y_tile[:, t % Y_SLOTS, :]).then_inc(y_stored[t % Y_SLOTS], 16)
                    if t + Y_SLOTS < TOKEN_TILES:
                        sp.wait_ge(y_stored[t % Y_SLOTS], signals_led(i, 32, 16))
                        y_load(t + Y_SLOTS)

            with sp.Fori(0, BATCH - 1) as i:
                batch(i, False)
            batch(BATCH - 1, True)
            for k in range(Y_SLOTS):
                sp.wait_ge(y_stored[k], signals_led(BATCH, 32, 0))

        @block.gpsimd
        def _(pool):
            nc.gpsimd.memset(identity[:, :], 0.0).then_inc(consts_ready, 1)
            nc.gpsimd.memset(minus_block[:, :, :], 0.0).then_inc(consts_ready, 1)
            pool.wait_ge(consts_ready, 2)
            nc.gpsimd.affine_select(out=identity[:, :], in_=identity[:, :], compare_op=ALU.not_equal, fill=1.0,
                                    base=0, pattern=[[-1, P]], channel_multiplier=1).then_inc(consts_ready, 1)
            nc.gpsimd.affine_select(out=minus_block[:, :, :], in_=minus_block[:, :, :], compare_op=ALU.not_equal,
                                    fill=-1.0, base=0, pattern=[[-1, Q_TILES], [0, P]],
                                    channel_multiplier=1).then_inc(consts_ready, 1)
            pool.wait_ge(bias_ready, 1)
            pool.sem_inc(p_lo_ready[POOL])
            pool.sem_inc(o_ready)
            with pool.Fori(0, BATCH) as i:
                def step_lo(s):
                    pool.wait_ge(exp_done, signals_led(i, KEYS_PER_STEP * STEPS, score_tiles(s)[-1] + 1))
                    pool.wait_ge(pv_done, signals_led(i, STEPS, max(s + 1 - P_SLOTS, 0)))
                    nc.gpsimd.tensor_tensor(p_lo[:, s % P_SLOTS, :, :], p_full[:, s % 2, :, :],
                                            p_hi[:, s % P_SLOTS, :, :], ALU.subtract).then_inc(p_lo_ready[POOL], 1)

                def normalise(u):
                    h, half = divmod(u, HALVES)
                    pool.wait_ge(o_free, signals_led(i, UNITS, u + 1))
                    nc.gpsimd.tensor_tensor(
                        o_heads[:, half * Q_TILES:(half + 1) * Q_TILES, h * DIM:(h + 1) * DIM], o_sum[:, :, :],
                        inv_sum[:, :].rearrange("p (t o) -> p t o", o=1).broadcast_to([P, Q_TILES, DIM]),
                        ALU.mult).then_inc(o_ready, 1)

                def y_bias(t):
                    pool.wait_ge(y_loaded[t % Y_SLOTS], signals(i, 32, 16 * (t // Y_SLOTS + 1)))
                    nc.gpsimd.tensor_tensor(y_tile[:, t % Y_SLOTS, :], y_tile[:, t % Y_SLOTS, :], out_bias[:, :],
                                            ALU.add).then_inc(y_biased, 1)

                for s in range(0, LAST_SLOT + 1):
                    if s >= 5 and s % STEPS_PER_UNIT == 1:
                        normalise((s - 5) // STEPS_PER_UNIT)
                    if s < STEPS and on_pool(s):
                        step_lo(s)
                    if s % STEPS_PER_UNIT == 2 and s // STEPS_PER_UNIT < Y_SLOTS:
                        y_bias(s // STEPS_PER_UNIT)
                for t in range(Y_SLOTS, TOKEN_TILES):
                    y_bias(t)

        @block.tensor
        def _(pe):
            pe.wait_ge(consts_ready, 4)
            pe.wait_ge(w_lo_done, 2 * TOKEN_TILES + CH_TILES)
            pe.wait_ge(fixed_ready, 1)
            for c in range(CH_TILES):
                cols = slice(c * P, (c + 1) * P)
                nc.tensor.matmul(psum[:, 5, :], bias_hi[:, cols], wout_hi[:, c, :], start=c == 0, stop=False)
                nc.tensor.matmul(psum[:, 5, :], bias_hi[:, cols], wout_lo[:, c, :], start=False, stop=False)
                last = nc.tensor.matmul(psum[:, 5, :], bias_lo[:, cols], wout_hi[:, c, :], start=False,
                                        stop=c == CH_TILES - 1)
            last.then_inc(bias_product, 1)

            pe.sem_inc(pv_done)

            with pe.Fori(0, BATCH) as i:
                def claim_fill(w):
                    before = last_in_bank(w)
                    if before is None and FILL_BANK[w] < SCORE_BANKS:
                        pe.wait_ge(exp_done, signals_led(i, KEYS_PER_STEP * STEPS, 0))
                    if before is not None:
                        pe.wait_ge(fill_done, signals_led(i, FILLS, FILL_AT[before] + 1))
                    elif FILL_BANK[w] == 3:
                        pe.wait_ge(fill_done, signals_led(i, FILLS, 0))
                    if before is None and FILL_BANK[w] >= 6:
                        pe.wait_ge(o_free, signals_led(i, UNITS, 0))
                    if before is None and FILL_BANK[w] in (4, 5):
                        pe.wait_ge(max_tile_done, signals_led(i, MAXES, MAXES))
                    return fill_bank(w)

                def claim_max(w):
                    n = MAX_AT[w]
                    if n < 2:
                        pe.wait_ge(fill_done, signals_led(i, FILLS, 0))
                    else:
                        pe.wait_ge(max_tile_done, signals_led(i, MAXES, n - 1))
                    return max_bank(w)

                def three_terms(a_hi, a_lo, b_hi, b_lo):
                    return [pair for c in range(CH_TILES) for pair in
                            ((a_hi(c), b_hi(c)), (a_hi(c), b_lo(c)), (a_lo(c), b_hi(c)))]

                def v_cols(w):
                    return lambda c: w[:, c, :].rearrange("p (h e) -> p h e", e=QKV)[:, :, 2 * DIM:QKV]

                def terms_of(w):
                    if w[0] == "qk":
                        toks = slice(w[2] * HALF, (w[2] + 1) * HALF)
                        cols = slice(w[1] * QKV, w[1] * QKV + 2 * DIM)
                        return three_terms(lambda c: wqkv_hi[:, c, cols], lambda c: wqkv_lo[:, c, cols],
                                           lambda c: xT_hi[:, c, toks], lambda c: xT_lo[:, c, toks])
                    toks = slice(w[1] * P, (w[1] + 1) * P)
                    left = lambda c: xT_hi[:, c, toks], lambda c: xT_lo[:, c, toks]
                    if w[0] == "v":
                        return three_terms(*left, v_cols(wqkv_hi), v_cols(wqkv_lo))
                    return three_terms(*left, lambda c: wout_hi[:, c, :], lambda c: wout_lo[:, c, :])

                def projection(w, first, last):
                    if first == 0:
                        claim_fill(w)
                        source = {"qk": lambda: ("x_transpose", 4 * w[2] + 3), "v": lambda: ("x_transpose", w[1]),
                                  "project": lambda: ("o_transpose", w[1])}[w[0]]()
                        pe.wait_ge(fill_done, signals_led(i, FILLS, FILL_AT[source] + 1))
                    for n, (a, b) in list(enumerate(terms_of(w)))[first:last]:
                        matmul = nc.tensor.matmul(fill_bank(w), a, b, start=n == 0, stop=n == TERMS - 1)
                    if last == TERMS:
                        matmul.then_inc(fill_ready, 1)

                def transpose(w):
                    dst, t = claim_fill(w), w[1]
                    if w[0] == "x_transpose":
                        pe.wait_ge(x_loaded[t % X_SLOTS], signals(i, 32, 16 * (t // X_SLOTS + 1)))
                        src = x_in[:, t % X_SLOTS, :]
                    else:
                        pe.wait_ge(o_ready, signals_led(i, UNITS, UNITS - 1 + t // Q_TILES))
                        src = o_heads[:, t, :]
                    for c in range(CH_TILES):
                        last = nc.tensor.transpose(dst[:, c * P:(c + 1) * P], src[:, c * P:(c + 1) * P], identity[:, :])
                    last.then_inc(fill_ready, 1)

                def fill(w, first=0, last=TERMS):
                    if w[0] in ("x_transpose", "o_transpose"):
                        transpose(w)
                    else:
                        projection(w, first, last)

                def row_max_tile(w):
                    _, u, q_tile, k_half = w
                    h, half = divmod(u, HALVES)
                    dst = claim_max(w)
                    pe.wait_ge(fill_done, signals_led(i, FILLS, FILL_AT["qk", h, 1] + 1))
                    pe.wait_ge(q_hi_hi_ready[half], signals(i, HEADS * 16, (h + 1) * 16))
                    q0 = half * HALF + q_tile * P
                    nc.tensor.matmul(dst, q_hi_hi[:, h % 2, q0:q0 + P],
                                     k_lo_hi[:, h % 2, k_half * HALF:(k_half + 1) * HALF],
                                     start=True, stop=True).then_inc(max_tile_ready, 1)

                def shift_tile(u):
                    dst = claim_max(("shift", u))
                    pe.wait_ge(max_ready, signals_led(i, UNITS, u + 1))
                    nc.tensor.transpose(dst[0:Q_TILES, 0:P], row_max[:, u % 2, :],
                                        identity[:, :]).then_inc(max_tile_ready, 1)

                def step_scores(s):
                    u = s // STEPS_PER_UNIT
                    h, half = divmod(u, HALVES)
                    if s == 0:
                        pe.wait_ge(fill_done, signals_led(i, FILLS, FILL_AT[BEFORE[-1]] + 1))
                    if s % STEPS_PER_UNIT == 0:
                        pe.wait_ge(max_tile_done, signals_led(i, MAXES, MAX_AT["shift", u] + 1))
                        if half == 0:
                            for k in range(HALVES):
                                pe.wait_ge(k_shift_ready[k], signals(i, HEADS * 16, (h + 1) * 16))
                    cols = slice(half * HALF, (half + 1) * HALF)
                    for n, tile in enumerate(score_tiles(s)):
                        pe.wait_ge(exp_done, signals_led(i, KEYS_PER_STEP * STEPS, max(tile + 1 - SCORE_BANKS, 0)))
                        keys = slice(key_tile(s, n) * P, (key_tile(s, n) + 1) * P)
                        nc.tensor.matmul(score_bank(tile), k_lo_hi[:, h % 2, keys], q_hi_hi[:, h % 2, cols],
                                         start=True, stop=False)
                        nc.tensor.matmul(score_bank(tile), k_shift[:, h % 2, keys], q_shift[:, h % 2, cols],
                                         start=False, stop=True).then_inc(scores_ready, 1)

                def step_pv(s):
                    u = s // STEPS_PER_UNIT
                    h = u // HALVES
                    if s == 0:
                        pe.wait_ge(fill_done, signals_led(i, FILLS, FILL_AT["v", TOKEN_TILES - 1] + 1))
                    if s % STEPS_PER_UNIT == 0:
                        pe.wait_ge(o_free, signals_led(i, UNITS, u))
                    pe.wait_ge(exp_done, signals_led(i, KEYS_PER_STEP * STEPS, score_tiles(s)[-1] + 1))
                    pe.wait_ge(p_lo_ready[on_pool(s)], signals_led(i, LOW_PARTS[on_pool(s)], low_parts(s)))
                    for n in range(KEYS_PER_STEP):
                        kt = key_tile(s, n)
                        for qt in range(Q_TILES):
                            bank, col = qt // 2, (qt % 2) * PV_W
                            qs = slice(qt * P, (qt + 1) * P)
                            nc.tensor.matmul(pv[:, bank, col:col + PV_W], p_hi[:, s % P_SLOTS, n, qs],
                                             v_parts[:, kt, h, 0:PV_W], start=kt == 0 and qt % 2 == 0,
                                             stop=False, skip_group_check=True)
                            last = nc.tensor.matmul(pv[:, bank, col + DIM:col + PV_W], p_lo[:, s % P_SLOTS, n, qs],
                                                    v_parts[:, kt, h, DIM:PV_W], start=False,
                                                    stop=kt == TOKEN_TILES - 1, skip_group_check=True)
                    last.then_inc(pv_done, 1)

                for w in BEFORE:
                    fill(w)
                for s in SLOTS:
                    if s == STEPS:
                        step_pv(s - 1)
                    for w in max_tiles_of_slot(s):
                        row_max_tile(w)
                    fills_after_scores = s >= 0 and s % STEPS_PER_HEAD == 0
                    if not fills_after_scores:
                        for part in fills_of_slot(s):
                            fill(*part)
                    if 0 <= s + 1 < STEPS:
                        step_scores(s + 1)
                    if fills_after_scores:
                        for part in fills_of_slot(s):
                            fill(*part)
                    for w in max_tiles_of_slot(s, late=True):
                        row_max_tile(w)
                    if shift_unit_of_slot(s) is not None:
                        shift_tile(shift_unit_of_slot(s))
                    if 1 <= s < STEPS:
                        step_pv(s - 1)
                for w in AFTER:
                    fill(w)

        @block.scalar
        def _(act):
            for n in range(2 * TOKEN_TILES):
                rnd, slot = divmod(n, 8)
                if slot == 0:
                    act.wait_ge(weights_in, 128 * (rnd + 1))
                if rnd == 0:
                    c, part = divmod(slot, 2)
                    dst = wqkv_hi[:, c, part * HALF:(part + 1) * HALF]
                elif slot < CH_TILES:
                    dst = wqkv_hi[:, slot, 2 * HALF:3 * HALF]
                else:
                    dst = wout_hi[:, slot - CH_TILES, :]
                nc.scalar.copy(dst, stage[:, slot, :]).then_inc(w_hi_done, 1)
            act.wait_ge(consts_in, 64)
            act.wait_ge(fixed_ready, 1)
            for c in range(CH_TILES):
                nc.scalar.activation(bias_hi[:, c * P:(c + 1) * P], zeros, ACT.Identity, bias=v_bias[:, c:c + 1]).then_inc(w_hi_done, 1)
            act.sem_inc(exp_done)

            with act.Fori(0, BATCH) as i:
                def transposed_hi(w):
                    t = w[1]
                    act.wait_ge(fill_ready, signals(i, FILLS, FILL_AT[w] + 1))
                    nc.scalar.copy(xT_hi[:, :, t * P:(t + 1) * P],
                                   fill_bank(w).rearrange("p (c k) -> p c k", c=CH_TILES)).then_inc(hi_done, 1)

                def qk_hi(w, matrices):
                    _, h, half = w
                    cols = slice(half * HALF, (half + 1) * HALF)
                    act.wait_ge(fill_ready, signals(i, FILLS, FILL_AT[w] + 1))
                    if "q" in matrices:
                        nc.scalar.activation(q_hi_hi[0:DIM, h % 2, cols], fill_bank(w)[0:DIM, :], ACT.Identity,
                                             bias=qk_bias[0:DIM, h:h + 1])
                    if "k" in matrices:
                        nc.scalar.activation(k_lo_hi[DIM:P, h % 2, cols], fill_bank(w)[DIM:P, :], ACT.Identity,
                                             bias=qk_bias[DIM:P, h:h + 1]).then_inc(hi_done, 1)

                def v_hi(w):
                    act.wait_ge(fill_ready, signals(i, FILLS, FILL_AT[w] + 1))
                    nc.scalar.copy(v_parts[:, w[1], :, DIM:2 * DIM],
                                   fill_bank(w).rearrange("p (h d) -> p h d", d=DIM)).then_inc(hi_done, 1)

                def take_hi(w, matrices="qk"):
                    if w[0] == "v":
                        v_hi(w)
                    elif w[0] == "qk":
                        qk_hi(w, matrices)
                    elif w[0] in ("x_transpose", "o_transpose"):
                        transposed_hi(w)

                def exp_tile(s, n):
                    tile = score_tiles(s)[n]
                    act.wait_ge(scores_ready, signals(i, KEYS_PER_STEP * STEPS, tile + 1))
                    if n == 0:
                        if s < 2:
                            for who in (False, True):
                                act.wait_ge(p_lo_ready[who], signals_led(i, LOW_PARTS[who], 0))
                        else:
                            act.wait_ge(p_lo_ready[on_pool(s - 2)],
                                        signals_led(i, LOW_PARTS[on_pool(s - 2)], low_parts(s - 2)))
                        act.wait_ge(pv_done, signals_led(i, STEPS, max(s + 1 - P_SLOTS, 0)))
                    nc.scalar.activation(p_full[:, s % 2, n, :], score_bank(tile), ACT.Exp, scale=SCALE, bias=prob_bias[:, :])
                    nc.scalar.activation(p_hi[:, s % P_SLOTS, n, :], score_bank(tile), ACT.Exp,
                                         scale=SCALE, bias=prob_bias[:, :]).then_inc(exp_done, 1)

                def unit_lo(u):
                    act.wait_ge(pv_done, signals_led(i, STEPS, STEPS_PER_UNIT * (u + 1)))
                    act.wait_ge(o_free, signals_led(i, UNITS, u))
                    nc.scalar.copy(o_lo[:, :, :].rearrange("p (b t) d -> p b t d", b=2),
                                   pv_columns(0, DIM)).then_inc(o_lo_ready, 1)

                for w in BEFORE:
                    take_hi(w)
                for s in SLOTS:
                    if 0 <= s < STEPS:
                        exp_tile(s, 0)
                    if 5 <= s < STEPS and s % STEPS_PER_UNIT == 1:
                        unit_lo((s - 5) // STEPS_PER_UNIT)
                    if s == STEPS:
                        unit_lo(UNITS - 1)
                    if 0 <= s < STEPS:
                        exp_tile(s, 1)
                    for part in high_parts_in_slot(s):
                        take_hi(*part)
                for w in AFTER:
                    take_hi(w)

        @block.vector
        def _(dve):
            nc.vector.memset(k_shift[0:DIM, :, :].bitcast(f32), 0.0).then_inc(zeroed, 1)
            nc.vector.memset(q_shift[0:DIM, :, :].bitcast(f32), 0.0)
            nc.vector.memset(v_parts[:, :, :, 2 * DIM:V_WIDTH], 1.0)
            nc.vector.memset(zeros, 0.0)
            nc.vector.memset(prob_bias[:, :], PROB_BIAS)
            dve.wait_ge(zeroed, 1)
            nc.vector.memset(k_shift[0:Q_TILES, :, :].bitcast(f32), 1.0).then_inc(fixed_ready, 1)
            for n in range(2 * TOKEN_TILES):
                rnd, slot = divmod(n, 8)
                dve.wait_ge(w_hi_done, n + 1)
                if rnd == 0:
                    c, part = divmod(slot, 2)
                    where = (slice(None), c, slice(part * HALF, (part + 1) * HALF))
                    hi, lo = wqkv_hi[where], wqkv_lo[where]
                elif slot < CH_TILES:
                    where = (slice(None), slot, slice(2 * HALF, 3 * HALF))
                    hi, lo = wqkv_hi[where], wqkv_lo[where]
                else:
                    hi, lo = wout_hi[:, slot - CH_TILES, :], wout_lo[:, slot - CH_TILES, :]
                nc.vector.tensor_tensor(lo, stage[:, slot, :], hi.bitcast(f32), ALU.subtract).then_inc(w_lo_done, 1)
            dve.wait_ge(consts_in, 64)
            for c in range(CH_TILES):
                dve.wait_ge(w_hi_done, 2 * TOKEN_TILES + c + 1)
                cols = slice(c * P, (c + 1) * P)
                nc.vector.tensor_scalar(bias_lo[:, cols], bias_hi[:, cols].bitcast(f32), v_bias[:, c:c + 1], -1.0,
                                        ALU.subtract, ALU.mult).then_inc(w_lo_done, 1)
            dve.wait_ge(bias_product, 1)
            nc.vector.tensor_tensor(out_bias[:, :], psum[:, 5, :], out_bias[:, :], ALU.add).then_inc(bias_ready, 1)
            dve.wait_ge(consts_ready, 4)
            for led in (fill_done, max_tile_done, p_lo_ready[DVE], o_free, max_ready):
                dve.sem_inc(led)
            with dve.Fori(0, BATCH) as i:
                def transposed_lo(w):
                    t = w[1]
                    dve.wait_ge(hi_done, signals(i, HIS, HI_AT[w] + 1))
                    toks = slice(t * P, (t + 1) * P)
                    nc.vector.tensor_tensor(xT_lo[:, :, toks], fill_bank(w).rearrange("p (c k) -> p c k", c=CH_TILES),
                                            xT_hi[:, :, toks].bitcast(f32), ALU.subtract).then_inc(fill_done, 1)

                def v_lo(w):
                    t = w[1]
                    dve.wait_ge(hi_done, signals(i, HIS, HI_AT[w] + 1))
                    nc.vector.tensor_tensor(v_parts[:, t, :, 0:DIM], fill_bank(w).rearrange("p (h d) -> p h d", d=DIM),
                                            v_parts[:, t, :, DIM:2 * DIM], ALU.subtract).then_inc(fill_done, 1)

                def qk_lo(w):
                    _, h, half = w
                    src = fill_bank(w)
                    dve.wait_ge(hi_done, signals(i, HIS, HI_AT[w] + 1))
                    cols = slice(half * HALF, (half + 1) * HALF)
                    nc.vector.scalar_tensor_tensor(k_lo_hi[0:DIM, h % 2, cols], src[DIM:P, :], qk_bias[DIM:P, h:h + 1],
                                                   k_lo_hi[DIM:P, h % 2, cols].bitcast(f32), ALU.add, ALU.subtract)
                    nc.vector.scalar_tensor_tensor(q_shift[DIM:P, h % 2, cols], src[0:DIM, :], qk_bias[0:DIM, h:h + 1],
                                                   q_hi_hi[0:DIM, h % 2, cols].bitcast(f32), ALU.add,
                                                   ALU.subtract).then_inc(fill_done, 1)

                def project_add(w):
                    t = w[1]
                    dve.wait_ge(y_biased, signals(i, TOKEN_TILES, t + 1))
                    y = y_tile[:, t % Y_SLOTS, :]
                    nc.vector.tensor_tensor(y, fill_bank(w), y, ALU.add).then_inc(fill_done, 1)

                def take(w):
                    dve.wait_ge(fill_ready, signals(i, FILLS, FILL_AT[w] + 1))
                    {"x_transpose": transposed_lo, "o_transpose": transposed_lo, "v": v_lo, "qk": qk_lo,
                     "project": project_add}[w[0]](w)

                def row_max_part(w):
                    _, u, q_tile, k_half = w
                    dve.wait_ge(max_tile_ready, signals(i, MAXES, MAX_AT[w] + 1))
                    if (q_tile, k_half) == (0, 0):
                        dve.wait_ge(max_ready, signals_led(i, UNITS, max(u - 1, 0)))
                    nc.vector.reduce_max(max_parts[:, u % 2, q_tile, k_half:k_half + 1], max_bank(w),
                                         AX.X).then_inc(max_tile_done, 1)

                def join_max(u):
                    dve.wait_ge(max_tile_done, signals_led(i, MAXES, MAX_AT["row_max", u, Q_TILES - 1, 1] + 1))
                    nc.vector.tensor_reduce(row_max[:, u % 2, :], max_parts[:, u % 2, :, :], AX.X,
                                            ALU.max).then_inc(max_ready, 1)

                def shift_rows(u):
                    h, half = divmod(u, HALVES)
                    w = ("shift", u)
                    dve.wait_ge(max_tile_ready, signals(i, MAXES, MAX_AT[w] + 1))
                    nc.vector.tensor_tensor(
                        q_shift[0:Q_TILES, h % 2, half * HALF:(half + 1) * HALF].rearrange("r (t q) -> r t q", q=P),
                        max_bank(w)[0:Q_TILES, 0:P].rearrange("r (o q) -> r o q", o=1).broadcast_to([Q_TILES, Q_TILES, P]),
                        minus_block[:, :, :], ALU.mult).then_inc(max_tile_done, 1)

                def step_lo(s):
                    dve.wait_ge(exp_done, signals_led(i, KEYS_PER_STEP * STEPS, score_tiles(s)[-1] + 1))
                    dve.wait_ge(pv_done, signals_led(i, STEPS, max(s + 1 - P_SLOTS, 0)))
                    nc.vector.tensor_tensor(p_lo[:, s % P_SLOTS, :, :], p_full[:, s % 2, :, :],
                                            p_hi[:, s % P_SLOTS, :, :], ALU.subtract).then_inc(p_lo_ready[DVE], 1)

                def unit_output(u):
                    dve.wait_ge(o_lo_ready, signals(i, UNITS, u + 1))
                    dve.wait_ge(o_ready, signals_led(i, UNITS, u))
                    nc.vector.reciprocal(inv_sum[:, :].rearrange("p (b t o) -> p b t o", b=2, o=1),
                                         pv_columns(2 * DIM, PV_W))
                    nc.vector.tensor_tensor(o_sum[:, :, :].rearrange("p (b t) d -> p b t d", b=2),
                                            pv_columns(DIM, 2 * DIM),
                                            o_lo[:, :, :].rearrange("p (b t) d -> p b t d", b=2),
                                            ALU.add).then_inc(o_free, 1)

                for w in BEFORE:
                    take(w)
                for s in SLOTS:
                    if s >= STEPS:
                        if s == STEPS:
                            unit_output(UNITS - 1)
                        for w in consumed_in_slot(s):
                            take(w)
                    for w in max_tiles_of_slot(s):
                        row_max_part(w)
                        if w[2:] == (Q_TILES - 1, 1):
                            join_max(w[1])
                    if s < 0:
                        for w in consumed_in_slot(s):
                            take(w)
                    if 5 <= s < STEPS and s % STEPS_PER_UNIT == 1:
                        unit_output((s - 5) // STEPS_PER_UNIT)
                    if 0 <= s < STEPS and not on_pool(s):
                        step_lo(s)
                    for w in max_tiles_of_slot(s, late=True):
                        row_max_part(w)
                        if w[2:] == (Q_TILES - 1, 1):
                            join_max(w[1])
                    if 0 <= s < STEPS:
                        for w in consumed_in_slot(s):
                            take(w)
                    if shift_unit_of_slot(s) is not None:
                        shift_rows(shift_unit_of_slot(s))
                for w in AFTER:
                    take(w)


_INPUTS = ["x", "L0_conv_w_qkv", "L0_conv_b_qkv", "L0_conv_w_out", "L0_conv_b_out"]


def kernel(**inputs):
    import numpy as np
    import concourse.bacc as bacc
    from concourse.bass_utils import run_bass_kernel_spmd

    nc = bacc.Bacc("TRN2", target_bir_lowering=False, num_devices=1)
    arrays, args = {}, []
    for name in _INPUTS:
        a = np.ascontiguousarray(inputs[name])
        arrays[f"in_{name}"] = a
        args.append(nc.dram_tensor(f"in_{name}", a.shape, mybir.dt.from_np(a.dtype), kind="ExternalInput").ap())
    result = nc.dram_tensor("result", (BATCH, HEIGHT, WIDTH, CH), mybir.dt.float32, kind="ExternalOutput").ap()
    attention_block(nc, *args, result)
    done = run_bass_kernel_spmd(nc, [arrays], core_ids=[0])
    return done.results[0]["result"]
```
